# Optimizing a Trainium2 kernel written in Bass

```python
import numpy as np
import jax
import jax.numpy as jnp

def _softmax(x, axis=-1):
    return jax.nn.softmax(x, axis=axis)

def _gelu(x):
    return jax.nn.gelu(x, approximate=True)

def _silu(x):
    return jax.nn.silu(x)

def _sigmoid(x):
    return jax.nn.sigmoid(x)

def _layernorm(x, axis=-1, eps=1e-05):
    m = jnp.mean(x, axis=axis, keepdims=True)
    v = jnp.var(x, axis=axis, keepdims=True)
    return (x - m) / jnp.sqrt(v + eps)

def _scatter_add(tgt, idx, src, axis=0):
    return tgt.at[idx].add(src)

def _segment_sum(src, seg, n):
    return jax.ops.segment_sum(src, seg, n)
kernel_name = 'mk_seq_postln_d1_jaxref_r4_19c1e3'

def setup_inputs(seed: int=0):
    np.random.seed(seed)
    _w = jnp.asarray

    def _L0_attn_setup():
        import jax, jax.numpy as jnp
        import numpy as np
        B, S, H_DIM = (2, 512, 512)
        N_HEADS, D_HEAD = (16, 128)
        key = jax.random.key(seed)
        k1, k2, k3 = jax.random.split(key, 3)
        x = jax.random.normal(k1, (B, S, H_DIM), dtype=jnp.float32)
        w_qkv = jax.random.normal(k2, (H_DIM, 3 * N_HEADS * D_HEAD), dtype=jnp.float32) * 0.02
        w_o = jax.random.normal(k3, (N_HEADS * D_HEAD, H_DIM), dtype=jnp.float32) * 0.02
        return {'x': x, 'w_qkv': w_qkv, 'w_o': w_o}
    _L0_attn_in = _L0_attn_setup()

    def _L0_ffn_setup():
        import math
        import jax, jax.numpy as jnp
        import numpy as np
        from jax import lax
        D = 512
        I = 256
        E = 32
        K = 4
        NG = 8
        TKG = 3
        NSH = 2
        SCALE = 2.5
        CF = 1.25
        B, S = (2, 512)

        def _router(x, router_w, e_bias):
            scores = jax.nn.sigmoid(x @ router_w.T)
            sc = scores + e_bias[None, :]
            T = x.shape[0]
            gs = sc.reshape(T, NG, E // NG)
            group_scores = lax.top_k(gs, 2)[0].sum(-1)
            _, gidx = lax.top_k(group_scores, TKG)
            gmask = jnp.zeros((T, NG), sc.dtype).at[jnp.arange(T)[:, None], gidx].set(1.0)
            smask = jnp.repeat(gmask, E // NG, axis=1)
            masked = jnp.where(smask > 0, sc, 0.0)
            _, topk_idx = lax.top_k(masked, K)
            topk_w = jnp.take_along_axis(scores, topk_idx, axis=1)
            topk_w = topk_w / (topk_w.sum(-1, keepdims=True) + 1e-20)
            topk_w = topk_w * SCALE
            return (topk_idx.astype(jnp.int32), topk_w)

        def _moe_forward(hidden_states, router_w, e_bias, W_gate, W_up, W_down, shared_gate, shared_up, shared_down):
            b, s, d = hidden_states.shape
            T = b * s
            C = int(math.ceil(CF * T / E))
            EC = E * C
            x = hidden_states.reshape(T, d)
            topk_idx, topk_w = _router(x, router_w, e_bias)
            expert_flat = topk_idx.reshape(-1)
            w_flat = topk_w.reshape(-1)
            tok_flat = jnp.repeat(jnp.arange(T, dtype=jnp.int32), K)
            sort_ix = jnp.argsort(expert_flat)
            e_sorted = expert_flat[sort_ix]
            tok_s = tok_flat[sort_ix]
            w_s = w_flat[sort_ix]
            counts = jnp.zeros(E, jnp.int32).at[e_sorted].add(1)
            group_start = jnp.concatenate([jnp.zeros(1, jnp.int32), jnp.cumsum(counts)[:-1].astype(jnp.int32)])
            pos = jnp.arange(T * K, dtype=jnp.int32) - group_start[e_sorted]
            valid = pos < C
            dest = e_sorted * C + jnp.where(valid, pos, 0)
            slots_token = jnp.zeros(EC, jnp.int32).at[dest].add(jnp.where(valid, tok_s, 0))
            slots_w = jnp.zeros(EC, w_s.dtype).at[dest].add(jnp.where(valid, w_s, 0.0))
            Xp = x[slots_token].reshape(E, C, d)
            G = jnp.einsum('ecd,edi->eci', Xp, W_gate)
            U = jnp.einsum('ecd,edi->eci', Xp, W_up)
            Y = jnp.einsum('eci,eid->ecd', jax.nn.silu(G) * U, W_down)
            Yf = Y.reshape(EC, d) * slots_w[:, None]
            out = jnp.zeros((T, d), x.dtype).at[slots_token].add(Yf)
            shared = jax.nn.silu(x @ shared_gate.T) * (x @ shared_up.T) @ shared_down.T
            return (out + shared).reshape(b, s, d)
        key = jax.random.key(seed)
        ks = jax.random.split(key, 8)

        def rn(k, shape, scale=0.02):
            return jax.random.normal(k, shape, jnp.float32) * scale
        return {'hidden_states': jax.random.normal(ks[0], (B, S, D), jnp.float32), 'router_w': rn(ks[1], (E, D)), 'e_bias': jnp.zeros((E,), jnp.float32), 'W_gate': rn(ks[2], (E, D, I)), 'W_up': rn(ks[3], (E, D, I)), 'W_down': rn(ks[4], (E, I, D)), 'shared_gate': rn(ks[5], (I * NSH, D)), 'shared_up': rn(ks[6], (I * NSH, D)), 'shared_down': rn(ks[7], (D, I * NSH))}
    _L0_ffn_in = _L0_ffn_setup()
    _d = {'L0_attn_x': _L0_attn_in['x'], 'L0_attn_w_qkv': _L0_attn_in['w_qkv'], 'L0_attn_w_o': _L0_attn_in['w_o'], 'L0_ffn_router_w': _L0_ffn_in['router_w'], 'L0_ffn_e_bias': _L0_ffn_in['e_bias'], 'L0_ffn_W_gate': _L0_ffn_in['W_gate'], 'L0_ffn_W_up': _L0_ffn_in['W_up'], 'L0_ffn_W_down': _L0_ffn_in['W_down'], 'L0_ffn_shared_gate': _L0_ffn_in['shared_gate'], 'L0_ffn_shared_up': _L0_ffn_in['shared_up'], 'L0_ffn_shared_down': _L0_ffn_in['shared_down']}
    _x0 = _d['L0_attn_x']
    _d['L0_attn_x'] = jax.random.normal(jax.random.fold_in(jax.random.key(seed), 1), (4, 1024, 512), dtype=_x0.dtype)
    del _x0
    return _d

def reference(L0_attn_x, L0_attn_w_qkv, L0_attn_w_o, L0_ffn_router_w, L0_ffn_e_bias, L0_ffn_W_gate, L0_ffn_W_up, L0_ffn_W_down, L0_ffn_shared_gate, L0_ffn_shared_up, L0_ffn_shared_down):

    def _L0_attn_ref(x, w_qkv, w_o):
        import jax, jax.numpy as jnp
        import numpy as np
        B, S, H_DIM = (2, 512, 512)
        N_HEADS, D_HEAD = (16, 128)
        b, s, _ = x.shape
        qkv = jnp.einsum('bsh,hf->bsf', x, w_qkv)
        qkv = qkv.reshape(b, s, 3, N_HEADS, D_HEAD)
        q, k, v = (qkv[:, :, 0], qkv[:, :, 1], qkv[:, :, 2])
        q = q.transpose(0, 2, 1, 3)
        k = k.transpose(0, 2, 1, 3)
        v = v.transpose(0, 2, 1, 3)
        scores = jnp.einsum('bhqd,bhkd->bhqk', q, k) / jnp.sqrt(jnp.float32(D_HEAD))
        probs = jax.nn.softmax(scores, axis=-1)
        values = jnp.einsum('bhqk,bhkd->bhkd', probs, v)
        values = values.transpose(0, 2, 1, 3).reshape(b, s, N_HEADS * D_HEAD)
        out = jnp.einsum('bsf,fh->bsh', values, w_o)
        return out

    def _L0_ffn_ref(hidden_states, router_w, e_bias, W_gate, W_up, W_down, shared_gate, shared_up, shared_down):
        import math
        import jax, jax.numpy as jnp
        import numpy as np
        from jax import lax
        D = 512
        I = 256
        E = 32
        K = 4
        NG = 8
        TKG = 3
        NSH = 2
        SCALE = 2.5
        CF = 1.25
        B, S = (2, 512)

        def _router(x, router_w, e_bias):
            scores = jax.nn.sigmoid(x @ router_w.T)
            sc = scores + e_bias[None, :]
            T = x.shape[0]
            gs = sc.reshape(T, NG, E // NG)
            group_scores = lax.top_k(gs, 2)[0].sum(-1)
            _, gidx = lax.top_k(group_scores, TKG)
            gmask = jnp.zeros((T, NG), sc.dtype).at[jnp.arange(T)[:, None], gidx].set(1.0)
            smask = jnp.repeat(gmask, E // NG, axis=1)
            masked = jnp.where(smask > 0, sc, 0.0)
            _, topk_idx = lax.top_k(masked, K)
            topk_w = jnp.take_along_axis(scores, topk_idx, axis=1)
            topk_w = topk_w / (topk_w.sum(-1, keepdims=True) + 1e-20)
            topk_w = topk_w * SCALE
            return (topk_idx.astype(jnp.int32), topk_w)

        def _moe_forward(hidden_states, router_w, e_bias, W_gate, W_up, W_down, shared_gate, shared_up, shared_down):
            b, s, d = hidden_states.shape
            T = b * s
            C = int(math.ceil(CF * T / E))
            EC = E * C
            x = hidden_states.reshape(T, d)
            topk_idx, topk_w = _router(x, router_w, e_bias)
            expert_flat = topk_idx.reshape(-1)
            w_flat = topk_w.reshape(-1)
            tok_flat = jnp.repeat(jnp.arange(T, dtype=jnp.int32), K)
            sort_ix = jnp.argsort(expert_flat)
            e_sorted = expert_flat[sort_ix]
            tok_s = tok_flat[sort_ix]
            w_s = w_flat[sort_ix]
            counts = jnp.zeros(E, jnp.int32).at[e_sorted].add(1)
            group_start = jnp.concatenate([jnp.zeros(1, jnp.int32), jnp.cumsum(counts)[:-1].astype(jnp.int32)])
            pos = jnp.arange(T * K, dtype=jnp.int32) - group_start[e_sorted]
            valid = pos < C
            dest = e_sorted * C + jnp.where(valid, pos, 0)
            slots_token = jnp.zeros(EC, jnp.int32).at[dest].add(jnp.where(valid, tok_s, 0))
            slots_w = jnp.zeros(EC, w_s.dtype).at[dest].add(jnp.where(valid, w_s, 0.0))
            Xp = x[slots_token].reshape(E, C, d)
            G = jnp.einsum('ecd,edi->eci', Xp, W_gate)
            U = jnp.einsum('ecd,edi->eci', Xp, W_up)
            Y = jnp.einsum('eci,eid->ecd', jax.nn.silu(G) * U, W_down)
            Yf = Y.reshape(EC, d) * slots_w[:, None]
            out = jnp.zeros((T, d), x.dtype).at[slots_token].add(Yf)
            shared = jax.nn.silu(x @ shared_gate.T) * (x @ shared_up.T) @ shared_down.T
            return (out + shared).reshape(b, s, d)
        return _moe_forward(hidden_states, router_w, e_bias, W_gate, W_up, W_down, shared_gate, shared_up, shared_down)
    x = L0_attn_x
    x = _layernorm(x + _L0_attn_ref(x, L0_attn_w_qkv, L0_attn_w_o), axis=-1)
    x = _layernorm(x + _L0_ffn_ref(x, L0_ffn_router_w, L0_ffn_e_bias, L0_ffn_W_gate, L0_ffn_W_up, L0_ffn_W_down, L0_ffn_shared_gate, L0_ffn_shared_up, L0_ffn_shared_down), axis=-1)
    return x

_drawn_inputs = setup_inputs


def setup_inputs(seed=0):
    import zlib

    import numpy as np

    out = dict(_drawn_inputs(seed))
    spreads = {'L0_ffn_e_bias': (0.0, 0.327)}
    factors = {'L0_ffn_router_w': 2.972,
     'L0_ffn_W_gate': 2.773,
     'L0_ffn_W_up': 2.702,
     'L0_ffn_W_down': 2.709}
    for name, (base, spread) in spreads.items():
        noise = np.random.default_rng([zlib.crc32(name.encode()), seed]).standard_normal(out[name].shape)
        drawn = base * np.exp(spread * noise) if base else spread * noise
        out[name] = jnp.asarray(drawn.astype(out[name].dtype))
    for name, factor in factors.items():
        out[name] = (out[name] * factor).astype(out[name].dtype)
    return out
```

```python
from contextlib import ExitStack

import concourse.bass as bass
from concourse import mybir

F32 = mybir.dt.float32
F32R = mybir.dt.float32r
U32 = mybir.dt.uint32
BF16 = mybir.dt.bfloat16
ALU = mybir.AluOpType
ACT = mybir.ActivationFunctionType
AX_X = mybir.AxisListType.X

P = 128
NB = 512
HI, LO = 0, 1
PASSES = ((HI, HI), (HI, LO), (LO, HI))


def wait(eng, sem, value):
    if not (isinstance(value, int) and value <= 0):
        eng.wait_ge(sem, value)


def attention(nc, x, xT, w_qkv, w_o, y):
    B, S, D = x.shape
    F = w_o.shape[0]
    DH = 128
    H = F // DH
    M = B * H
    C = D // P
    T = S // P
    HALVES = S // NB
    PAIRS = M // 2
    PB = H // 2
    SCALE = float(DH) ** -0.5
    Q, K, V = range(3)
    G = 3 * HALVES
    assert T == 8 and HALVES == 2 and PB == T and C == 4

    with ExitStack() as ctx:
        def sb(name, shape, dt=F32):
            return ctx.enter_context(nc.sbuf_tensor(name, shape, dt))

        def sem(name):
            return ctx.enter_context(nc.semaphore(name))

        xt = sb("xt", [P, 2, 2, C, S], F32R)
        x_raw = sb("x_raw", [P, 2, C, P])
        y_sb = sb("y_sb", [P, T, D])
        w_raw = sb("w_raw", [P, 3, C, DH])
        w_sb = sb("w_sb", [P, 2, 3, C, DH], F32R)
        wo_raw = sb("wo_raw", [P, 2, D])
        wo_sb = sb("wo_sb", [P, 2, 2, D], F32R)
        qk = sb("qk", [P, 2, 2, 2, S], F32R)
        ex = sb("ex", [P, 2, S])
        colsum = sb("colsum", [P, S])
        cs = sb("cs", [P, 2, S], F32R)
        v_sb = sb("v_sb", [P, 2, S])
        val = sb("val", [P, 2, S])
        val2 = sb("val2", [P, 2, 2, S], F32R)
        ones_f = sb("ones_f", [P, P])
        ones = sb("ones", [P, P], F32R)
        neg_max = sb("neg_max", [P, 2, 1])
        rowsum = sb("rowsum", [P, 2, 1])
        inv = sb("inv", [P, 2, 1])
        first_x = [x_raw[:, k] for k in range(2)]
        for buf in (ex, val):
            first_x += [buf[:, a, b * NB:b * NB + NB].rearrange("p (c t) -> p c t", c=C)
                        for a in range(2) for b in range(HALVES)]
        p_s = ctx.enter_context(nc.psum_tensor("p_s", [P, 2, S], F32))
        p_g = ctx.enter_context(nc.psum_tensor("p_g", [P, 2, NB], F32))
        p_o = ctx.enter_context(nc.psum_tensor("p_o", [P, 2, NB], F32))

        in_w = [sem(f"in_w{r}") for r in range(3)]
        in_wo = [sem(f"in_wo{r}") for r in range(2)]
        in_x = [sem(f"in_x{r}") for r in range(2)]
        in_y = [sem(f"in_y{j}") for j in range(T)]
        out_y = [sem(f"out_y{j}") for j in range(T)]
        pe_s = sem("pe_s")
        pe_g = sem("pe_g")
        pe_cs = sem("pe_cs")
        pe_o = sem("pe_o")
        act_e = sem("act_e")
        act_g = sem("act_g")
        act_cs = sem("act_cs")
        act_val = sem("act_val")
        act_w = sem("act_w")
        act_wo = sem("act_wo")
        act_x = sem("act_x")
        dve_m = sem("dve_m")
        dve_r = sem("dve_r")
        dve_p = sem("dve_p")
        dve_g = sem("dve_g")
        dve_cs = sem("dve_cs")
        dve_v = sem("dve_v")
        dve_val = sem("dve_val")
        dve_y = sem("dve_y")
        dve_1 = sem("dve_1")
        pool_w = sem("pool_w")
        pool_wo = sem("pool_wo")
        pool_x = sem("pool_x")

        def rounded(tile):
            return tile.bitcast(F32)

        def xt_part(par, part, c, at, size):
            whole = xt[:].rearrange("p a h c t -> p (a h c t)")
            return whole[:, bass.ds(par * (2 * C * S) + at + (part * C * S + c * S), size)]

        w_dram = w_qkv.rearrange("(c p) (r h f) -> p r h c f", p=P, r=3, f=DH)
        wo_dram = w_o.rearrange("(h p) d -> p h d", p=P)
        xT_dram = xT.rearrange("(c p) (n t) -> p n c t", p=P, t=P)
        x_rows = x.rearrange("b (j p) d -> p b j d", p=P)
        y_rows = y.rearrange("(b j p) d -> p b j d", p=P, j=T)

        def flat1(ap, names="p o d -> p (o d)"):
            return ap.rearrange(names)

        block = ctx.enter_context(nc.Block())

        @block.sync
        def _(sp):
            def load_w(h, m, first=False):
                for r in range(3):
                    wait(sp, act_w, 3 * (m - 1) + r + 1)
                    wait(sp, pool_w, 3 * (m - 1) + r + 1)
                    src = w_dram[:, r, bass.ds(h, 1)].rearrange("p o c f -> p (o c) f")
                    sp.dma_start(w_raw[:, r], src).then_inc(in_w[r], 16)

            def load_wo(h, m, r):
                wait(sp, act_wo, m - 1)
                wait(sp, pool_wo, m - 1)
                sp.dma_start(wo_raw[:, r], wo_dram[:, bass.ds(h, 1)].rearrange("p o d -> p (o d)"))\
                    .then_inc(in_wo[r], 16)

            def load_x(k, r, split):
                wait(sp, act_x, split)
                wait(sp, pool_x, split)
                sp.dma_start(x_raw[:, r], xT_dram[:, bass.ds(k, 1)].rearrange("p o c t -> p (o c) t"))\
                    .then_inc(in_x[r], 16)

            def pair(b, k, last=False, more_x=True, first=False):
                i = b * PB + k
                for s in range(2):
                    n = 2 * i + s
                    if not last:
                        load_w((2 * k + s + 2) % H if isinstance(k, int) else 2 * k + (s + 2), n + 2)
                    load_wo(2 * k + s, n, s)
                    if s == 0 and more_x:
                        load_x(T + i, 0, T + i)
                    if k_is(k, 0) and not first:
                        swap(b, s)

            def k_is(k, v):
                return isinstance(k, int) and k == v

            def swap(b, s):
                for j in range(4 * s, 4 * s + 4):
                    wait(sp, dve_y, (b * PB - 1) * T + j + 1)
                    store_y(b - 1, j)
                for j in range(4 * s, 4 * s + 4):
                    wait(sp, out_y[j], 16 * b)
                    load_y(b, j)

            def store_y(b, j):
                sp.dma_start(y_rows[:, bass.ds(b, 1), j].rearrange("p o d -> p (o d)"), y_sb[:, j])\
                    .then_inc(out_y[j], 16)

            def load_y(b, j):
                sp.dma_start(y_sb[:, j], x_rows[:, bass.ds(b, 1), j].rearrange("p o d -> p (o d)"))\
                    .then_inc(in_y[j], 16)

            for k in range(T):
                sp.dma_start(first_x[k], xT_dram[:, k]).then_inc(in_x[k % 2], 16)
                if k == 0:
                    load_w(0, 0)
            load_w(1, 1)
            for j in range(T):
                load_y(0, j)
            pair(0, 0, first=True)
            with sp.Fori(1, PB - 1) as k:
                pair(0, k)
            pair(0, PB - 1)
            with sp.Fori(1, B - 1) as b:
                pair(b, 0)
                with sp.Fori(1, PB - 1) as k:
                    pair(b, k)
                pair(b, PB - 1)
            pair(B - 1, 0, more_x=False)
            with sp.Fori(1, PB - 1) as k:
                pair(B - 1, k, more_x=False)
            pair(B - 1, PB - 1, last=True, more_x=False)
            for j in range(T):
                wait(sp, dve_y, (PAIRS - 1) * T + j + 1)
                store_y(B - 1, j)
            for j in range(T):
                wait(sp, out_y[j], 16 * B)

        def pairs(eng, pair):
            pair(0)
            pair(1)
            with eng.Fori(2, (B - 1) * PB) as i:
                pair(i)
            with eng.Fori((B - 1) * PB, PAIRS - 1) as i:
                pair(i, more_x=False)
            pair(PAIRS - 1, more_x=False)

        def is_last(i):
            return isinstance(i, int) and i == PAIRS - 1

        def is_first(i):
            return isinstance(i, int) and i == 0

        def x_piece(k):
            return (k >> 3) & 1, (k & 7) * P

        @block.gpsimd
        def _(pool):
            def lo_w(m, r):
                wait(pool, act_w, 3 * m + r + 1)
                pool.tensor_tensor(w_sb[:, LO, r], w_raw[:, r], rounded(w_sb[:, HI, r]), ALU.subtract)\
                    .then_inc(pool_w, 1)

            def lo_wo(m, r):
                wait(pool, act_wo, m + 1)
                pool.tensor_tensor(wo_sb[:, r, LO], wo_raw[:, r], rounded(wo_sb[:, r, HI]), ALU.subtract)\
                    .then_inc(pool_wo, 1)

            def lo_x(k, r):
                wait(pool, act_x, k + 1)
                par, at = x_piece(k)
                for c in range(C):
                    ins = pool.tensor_tensor(xt_part(par, LO, c, at, P), x_raw[:, r, c],
                                             rounded(xt_part(par, HI, c, at, P)), ALU.subtract)
                ins.then_inc(pool_x, 1)

            def pair(i, more_x=True):
                for s in range(2):
                    n = 2 * i + s
                    if s == 0 and not is_first(i):
                        lo_wo(n - 2, 0)
                    if not is_last(i):
                        lo_w(n + 2, Q)
                    if s == 0 and not is_first(i):
                        lo_wo(n - 1, 1)
                    if not is_last(i):
                        lo_w(n + 2, K)
                    if s == 0 and more_x:
                        lo_x(T + i, 0)
                    if not is_last(i):
                        lo_w(n + 2, V)

            for m in range(2):
                for r in range(3):
                    lo_w(m, r)
            pairs(pool, pair)
            lo_wo(M - 2, 0)
            lo_wo(M - 1, 1)

        @block.scalar
        def _(act):
            def hi_w(m, r):
                wait(act, in_w[r], 16 * (m + 1))
                wait(act, pe_g, G * (m - 1) + 2 * r + 2)
                act.copy(w_sb[:, HI, r], w_raw[:, r]).then_inc(act_w, 1)

            def hi_wo(m, r, i):
                wait(act, in_wo[r], 16 * i)
                wait(act, pe_o, T * (i - 1))
                act.copy(wo_sb[:, r, HI], wo_raw[:, r]).then_inc(act_wo, 1)

            def hi_x(k, r, loaded, heads):
                wait(act, in_x[r], 16 * loaded)
                wait(act, pe_g, G * heads)
                par, at = x_piece(k)
                for c in range(C):
                    ins = act.copy(xt_part(par, HI, c, at, P), x_raw[:, r, c])
                ins.then_inc(act_x, 1)

            def hi_g(m, par, g):
                r, half = divmod(g, 2)
                at = slice(half * NB, half * NB + NB)
                wait(act, pe_g, G * m + g + 1)
                if r == V:
                    if g == 4:
                        wait(act, dve_v, 2 * (m - 1))
                    act.copy(v_sb[:, par, at], p_g[:, g % 2]).then_inc(act_g, 1)
                else:
                    if g == 0:
                        wait(act, pe_s, T * (m - 1))
                    act.activation(qk[:, par, r, HI, at], p_g[:, g % 2], ACT.Copy,
                                   scale=SCALE if r == Q else 1.0).then_inc(act_g, 1)

            def hi_cs(m):
                wait(act, dve_p, T * (m + 1))
                wait(act, pe_cs, 2 * m)
                act.copy(cs[:, HI], colsum[:]).then_inc(act_cs, 1)

            def hi_val(m, r, i):
                wait(act, dve_v, 2 * (m + 1))
                wait(act, pe_o, T * (i - 1))
                act.copy(val2[:, r, HI], val[:, r]).then_inc(act_val, 1)

            def exp_tile(n, t):
                tau = n * T + t
                wait(act, dve_m, tau + 1)
                wait(act, dve_p, tau - 1)
                act.activation(ex[:, t % 2], p_s[:, t % 2], ACT.Exp, bias=neg_max[:, t % 2],
                               accum_out=rowsum[:, t % 2]).then_inc(act_e, 1)

            def pair(i, more_x=True):
                for s in range(2):
                    n = 2 * i + s
                    project = not (is_last(i) and s == 1)
                    for t in range(T):
                        if 1 <= t <= 6 and project:
                            hi_g(n + 1, 1 - s, t - 1)
                        if t == 1 and not (is_first(i) and s == 0):
                            hi_cs(n - 1)
                        if s == 0 and not is_first(i):
                            if t == 1:
                                hi_wo(n - 2, 0, i)
                            if t == 2:
                                hi_val(n - 2, 0, i)
                            if t == 4:
                                hi_wo(n - 1, 1, i)
                            if t == 5:
                                hi_val(n - 1, 1, i)
                        if t in (3, 5, 7) and not is_last(i):
                            hi_w(n + 2, (t - 3) // 2)
                        if t == 6 and s == 0 and more_x:
                            hi_x(T + i, 0, T // 2 + i + 1, H * (i >> 3) + 1)
                        exp_tile(n, t)

            for k in range(T):
                wait(act, in_x[k % 2], 16 * (T // 2))
                act.copy(xt[:, 0, HI, :, k * P:k * P + P], first_x[k]).then_inc(act_x, 1)
                if k < 3:
                    hi_w(0, k)
            for g in range(2):
                hi_g(0, 0, g)
            hi_w(1, Q)
            for g in range(2, 4):
                hi_g(0, 0, g)
            hi_w(1, K)
            for g in range(4, 6):
                hi_g(0, 0, g)
            hi_w(1, V)
            pairs(act, pair)
            hi_cs(M - 1)
            hi_wo(M - 2, 0, PAIRS)
            hi_wo(M - 1, 1, PAIRS)
            hi_val(M - 2, 0, PAIRS)
            hi_val(M - 1, 1, PAIRS)

        @block.vector
        def _(dve):
            def max_tile(n, t):
                wait(dve, pe_s, n * T + t + 1)
                dve.tensor_reduce(neg_max[:, t % 2], p_s[:, t % 2], AX_X, ALU.max, negate=True)\
                    .then_inc(dve_m, 1)

            def add_tile(n, t):
                tau = n * T + t
                wait(dve, act_e, tau + 1)
                dve.reciprocal(inv[:, t % 2], rowsum[:, t % 2]).then_inc(dve_r, 1)
                wait(dve, dve_r, tau + 1)
                if t == 0:
                    wait(dve, act_cs, n)
                    wait(dve, dve_cs, n)
                    dve.tensor_scalar(colsum[:], ex[:, 0], inv[:, 0], None, ALU.mult).then_inc(dve_p, 1)
                else:
                    wait(dve, dve_p, tau)
                    dve.scalar_tensor_tensor(out=colsum[:], in0=ex[:, t % 2], scalar=inv[:, t % 2],
                                             in1=colsum[:], op0=ALU.mult, op1=ALU.add).then_inc(dve_p, 1)

            def lo_g(m, par, g):
                r, half = divmod(g, 2)
                at = slice(half * NB, half * NB + NB)
                wait(dve, act_g, G * m + g + 1)
                dve.scalar_tensor_tensor(out=qk[:, par, r, LO, at], in0=p_g[:, g % 2],
                                         scalar=SCALE if r == Q else 1.0,
                                         in1=rounded(qk[:, par, r, HI, at]),
                                         op0=ALU.mult, op1=ALU.subtract).then_inc(dve_g, 1)

            def lo_cs(m):
                wait(dve, act_cs, m + 1)
                dve.tensor_tensor(cs[:, LO], colsum[:], rounded(cs[:, HI]), ALU.subtract).then_inc(dve_cs, 1)

            def times_v(m, par):
                wait(dve, act_g, G * (m + 1))
                wait(dve, act_val, m - 1)
                wait(dve, dve_val, m - 1)
                for half in range(2):
                    at = slice(half * NB, half * NB + NB)
                    wait(dve, pe_cs, 2 * m + half + 1)
                    dve.tensor_tensor(val[:, par, at], v_sb[:, par, at], p_o[:, half], ALU.mult)\
                        .then_inc(dve_v, 1)

            def lo_val(m, r):
                wait(dve, act_val, m + 1)
                dve.tensor_tensor(val2[:, r, LO], val[:, r], rounded(val2[:, r, HI]), ALU.subtract)\
                    .then_inc(dve_val, 1)

            def add_y(i, j):
                wait(dve, pe_o, T * (i - 1) + j + 1)
                wait(dve, in_y[j], 16 * (((i - 1) >> 3) + 1))
                dve.tensor_tensor(y_sb[:, j], y_sb[:, j], p_o[:, j % 2], ALU.add).then_inc(dve_y, 1)

            def pair(i, more_x=True):
                for s in range(2):
                    n = 2 * i + s
                    project = not (is_last(i) and s == 1)
                    for t in range(T):
                        if t == 7 and not is_first(i):
                            add_y(i, 4 * s)
                            add_y(i, 4 * s + 1)
                        if t == 0:
                            if s == 0 and not (isinstance(i, int) and i <= 1):
                                add_y(i - 1, 6)
                                add_y(i - 1, 7)
                            if s == 1 and not is_first(i):
                                add_y(i, 2)
                                add_y(i, 3)
                        max_tile(n, t)
                        if t == 0 and not (is_first(i) and s == 0):
                            add_tile(n - 1, T - 1)
                        if 1 <= t <= 4 and project:
                            lo_g(n + 1, 1 - s, t - 1)
                        if t == 1 and not (is_first(i) and s == 0):
                            lo_cs(n - 1)
                        if t == 3 and not (is_first(i) and s == 0):
                            times_v(n - 1, 1 - s)
                        if s == 0 and not is_first(i):
                            if t == 2:
                                lo_val(n - 2, 0)
                            if t == 5:
                                lo_val(n - 1, 1)
                        if t >= 1:
                            add_tile(n, t - 1)

            dve.memset(ones_f[:], 1.0).then_inc(dve_1, 1)
            dve.wait_ge(dve_1, 1)
            dve.tensor_copy(ones[:], ones_f[:]).then_inc(dve_1, 1)
            for k in range(T):
                at = slice(k * P, k * P + P)
                wait(dve, act_x, k + 1)
                dve.tensor_tensor(xt[:, 0, LO, :, at], first_x[k], rounded(xt[:, 0, HI, :, at]),
                                  ALU.subtract).then_inc(pool_x, 1)
            for g in range(4):
                lo_g(0, 0, g)
            pairs(dve, pair)
            add_tile(M - 1, T - 1)
            add_y(PAIRS - 1, 6)
            add_y(PAIRS - 1, 7)
            lo_cs(M - 1)
            times_v(M - 1, 1)
            lo_val(M - 2, 0)
            lo_val(M - 1, 1)
            for j in range(T):
                add_y(PAIRS, j)

        @block.tensor
        def _(pe):
            def project(m, par, g, batch_par):
                r, half = divmod(g, 2)
                wait(pe, pool_w, 3 * m + r + 1)
                wait(pe, act_g, G * m + g - 1)
                if g >= 2:
                    wait(pe, dve_g, 4 * m + g - 1)
                for c in range(C):
                    for a, b in PASSES:
                        ins = pe.matmul(p_g[:, g % 2], w_sb[:, a, r, c],
                                        xt_part(batch_par, b, c, half * NB, NB),
                                        start=(c == 0 and (a, b) == PASSES[0]),
                                        stop=(c == C - 1 and (a, b) == PASSES[-1]))
                ins.then_inc(pe_g, 1)

            def scores(n, par, t):
                if t == 0:
                    wait(pe, dve_g, 4 * (n + 1))
                wait(pe, act_e, n * T + t - 1)
                at = slice(t * P, t * P + P)
                for a, b in PASSES:
                    for half in range(HALVES):
                        keys = slice(half * NB, half * NB + NB)
                        ins = pe.matmul(p_s[:, t % 2, keys], qk[:, par, Q, a, at], qk[:, par, K, b, keys],
                                        start=((a, b) == PASSES[0]), stop=((a, b) == PASSES[-1]))
                ins.then_inc(pe_s, 1)

            def spread(m):
                wait(pe, dve_cs, m + 1)
                for half in range(HALVES):
                    at = slice(half * NB, half * NB + NB)
                    for part in (HI, LO):
                        ins = pe.matmul(p_o[:, half], ones[:], cs[:, part, at],
                                        start=(part == HI), stop=(part == LO))
                    ins.then_inc(pe_cs, 1)

            def out_tile(i, j):
                wait(pe, dve_val, 2 * i)
                wait(pe, pool_wo, 2 * i)
                if j % 4 >= 2:
                    wait(pe, dve_y, T * (i - 1) + j - 1)
                at = slice(j * P, j * P + P)
                for r in range(2):
                    for a, b in PASSES:
                        ins = pe.matmul(p_o[:, j % 2], val2[:, r, a, at], wo_sb[:, r, b],
                                        start=(r == 0 and (a, b) == PASSES[0]),
                                        stop=(r == 1 and (a, b) == PASSES[-1]))
                ins.then_inc(pe_o, 1)

            def pair(i, more_x=True):
                for s in range(2):
                    n = 2 * i + s
                    batch_par = ((i + s) >> 3) & 1
                    for t in range(T):
                        scores(n, s, t)
                        if t == 0 and not (is_last(i) and s == 1):
                            wait(pe, pool_x, T * (((i + s) >> 3) + 1))
                        if t < G and not (is_last(i) and s == 1):
                            project(n + 1, 1 - s, t, batch_par)
                        if t == 2 and not (is_first(i) and s == 0):
                            if not is_first(i):
                                wait(pe, dve_y, T * (i - 1) if s == 0 else T * (i - 1) + 4)
                            spread(n - 1)
                        if t >= 6 and not is_first(i):
                            if t == 6:
                                wait(pe, dve_v, 2 * n)
                            out_tile(i, 4 * s + 2 * (t - 6))
                            out_tile(i, 4 * s + 2 * (t - 6) + 1)

            for g in range(G):
                if g < 2:
                    wait(pe, pool_x, T // 2 * (g + 1))
                project(0, 0, g, 0)
            pe.wait_ge(dve_1, 2)
            pair(0)
            pair(1)
            with pe.Fori(2, PAIRS - 1) as i:
                pair(i)
            pair(PAIRS - 1)
            pe.wait_ge(dve_y, T * (PAIRS - 1))
            spread(M - 1)
            pe.wait_ge(dve_v, 2 * M)
            for j in range(T):
                if j in (4, 5):
                    pe.wait_ge(dve_y, T * (PAIRS - 1) + j - 1)
                out_tile(PAIRS, j)


class Chain:

    def __init__(self, eng, sem, per):
        self.eng, self.sem, self.per, self.base, self.n = eng, sem, per, 0, 0

    def turn(self, k):
        self.base, self.n = k * self.per, 0

    def then(self, ins):
        ins.then_inc(self.sem, 1)
        self.n += 1

    def settle(self):
        self.eng.wait_ge(self.sem, self.base + self.n)

    def settle_idle(self, spare):
        self.settle()
        self.eng.memset(spare, 0.0)

    def step(self, ins):
        self.then(ins)
        self.settle()

    def close(self):
        assert self.n == self.per, (self.n, self.per)


RSQRT_SEED = 0x5F3759DF
NEWTON = 3


def ln_rsqrt(dve, link, eps, var, v, g, a):
    link.step(dve.tensor_scalar(v, var, eps, None, ALU.add))
    link.step(dve.tensor_scalar(a.bitcast(U32), v.bitcast(U32), 1, None, ALU.logical_shift_right))
    link.step(dve.tensor_scalar(g.bitcast(U32), a.bitcast(U32), -1.0, float(RSQRT_SEED), ALU.mult, ALU.add))
    for _ in range(NEWTON):
        link.step(dve.scalar_tensor_tensor(out=a, in0=g, scalar=-0.5, in1=g, op0=ALU.mult, op1=ALU.mult))
        link.step(dve.tensor_tensor(a, a, v, ALU.mult))
        link.step(dve.scalar_tensor_tensor(out=g, in0=a, scalar=1.5, in1=g, op0=ALU.add, op1=ALU.mult))


LN_LINKS = 2 * 4 + 3 + 3 * NEWTON


def layernorm4(dve, link, eps, src, dst, bn, mv, small, spare):
    for j in range(4):
        link.then(dve.bn_stats(bn[:, j], src[:, j]))
    link.settle_idle(spare)
    for j in range(4):
        link.then(dve.bn_aggr(mv[:, j], bn[:, j]))
    link.settle()
    ln_rsqrt(dve, link, eps, mv[:, :, 1], small[:, 0], small[:, 1], small[:, 2])
    return [dve.tensor_scalar(dst[:, j], src[:, j], mv[:, j, 0:1], small[:, 1, j:j + 1],
                              ALU.subtract, ALU.mult) for j in range(4)]


def route_and_share(nc, ident, y, router_wT, e_bias, gate_T, up_T, down_T, x2, acc, table, C_SLOTS):
    N, D = y.shape
    E = router_wT.shape[1]
    I = gate_T.shape[1]
    KC, IC = D // P, I // P
    TT = NB // P
    TURNS = N // NB
    TOPK, NG, TKG, GE, ROUTED = 4, 8, 3, E // 8, 2.5
    HALF = C_SLOTS // 2
    COLS = 2 * E
    NOBODY = 2.0 * N
    assert KC == 4 and IC == 4 and GE == 4

    with ExitStack() as ctx:
        def sb(name, shape, dt=F32):
            return ctx.enter_context(nc.sbuf_tensor(name, shape, dt))

        def ps(name, shape):
            return ctx.enter_context(nc.psum_tensor(name, shape, F32))

        def sem(name):
            return ctx.enter_context(nc.semaphore(name))

        def rounded(tile):
            return tile.bitcast(F32)

        r_raw = sb("r_raw", [P, KC, E])
        r_sb = sb("r_sb", [P, 2, KC, E], F32R)
        s_raw = sb("s_raw", [P, 3, KC, I])
        s_sb = sb("s_sb", [P, 2, 3, KC, I], F32R)
        yb = sb("yb", [P, 2, TT, D])
        xb = sb("xb", [P, 2, TT, D])
        xT2 = sb("xT2", [P, 2, 2, KC, NB], F32R)
        sg = sb("sg", [P, 2, NB])
        hf = sb("hf", [P, 2, NB])
        hb = sb("hb", [P, 2, IC, NB], F32R)
        ab = sb("ab", [P, TT, D])
        before = sb("before", [P, P], BF16)
        every = sb("every", [P, P], BF16)
        iota_e = sb("iota_e", [P, E])
        iota_g = sb("iota_g", [P, NG])
        bias = sb("bias", [P, E])
        empty = sb("empty", [P, COLS * HALF // P, 2])
        bn = sb("bn", [P, TT, 6])
        mv = sb("mv", [P, TT, 2])
        small = sb("small", [P, 3, TT])
        spare = sb("spare", [P, 1])
        idle = sb("idle", [P, 1])
        prob = sb("prob", [P, TT, E])
        sc = sb("sc", [P, TT, E])
        pair_hi = sb("pair_hi", [P, TT * NG, 2])
        pair_lo = sb("pair_lo", [P, TT * NG, 2])
        top1 = sb("top1", [P, TT * NG])
        top2 = sb("top2", [P, TT * NG])
        top2b = sb("top2b", [P, TT * NG])
        gscore = sb("gscore", [P, TT, NG])
        g8 = sb("g8", [P, TT, 8])
        gi = sb("gi", [P, TT, 8], U32)
        g_hot = sb("g_hot", [P, TT, TKG, NG])
        g_mask = sb("g_mask", [P, TT, NG])
        masked = sb("masked", [P, TT, E])
        e8 = sb("e8", [P, TT, 8])
        ei = sb("ei", [P, TT, 8], U32)
        hot = sb("hot", [P, TT, TOPK, E])
        chosen = sb("chosen", [P, TT, E], BF16)
        tmp = sb("tmp", [P, TT, TOPK, E])
        wk = sb("wk", [P, TT, TOPK])
        wsum = sb("wsum", [P, TT])
        winv = sb("winv", [P, TT])
        taken = sb("taken", [P, E])
        pos = sb("pos", [P, TT, E])
        pos_k = sb("pos_k", [P, TT, TOPK])
        second = sb("second", [P, TT, TOPK])
        column = sb("column", [P, TT, TOPK])
        slot = sb("slot", [P, 2, TT, TOPK], U32)
        token = sb("token", [P, TT, TOPK])
        entry = sb("entry", [P, 2, TT, TOPK, 2])

        p_t = ps("p_t", [P, 2, KC, P])
        p_r = ps("p_r", [P, NB])
        p_c = ps("p_c", [P, NB])
        p_f = ps("p_f", [P, 2, 2, NB])

        in_r = sem("in_r")
        in_s = [sem(f"in_s{r}") for r in range(3)]
        in_b = sem("in_b")
        in_yb = [sem(f"in_yb{r}") for r in range(2)]
        out_e = sem("out_e")
        out_x = [sem(f"out_x{r}") for r in range(2)]
        out_a = sem("out_a")
        out_t = [sem(f"out_t{r}") for r in range(2)]
        act_s = sem("act_s")
        dve_s = sem("dve_s")
        pool_c = sem("pool_c")
        pool_i = sem("pool_i")
        ln_c = sem("ln_c")
        ro_c = sem("ro_c")
        dve_ln = sem("dve_ln")
        pe_t = sem("pe_t")
        act_t = sem("act_t")
        dve_t = sem("dve_t")
        pe_r = sem("pe_r")
        act_r = sem("act_r")
        dve_m = sem("dve_mm")
        pe_c = sem("pe_c")
        dve_e = sem("dve_e")
        pe_f = sem("pe_f")
        act_f = sem("act_f")
        dve_f1 = sem("dve_f1")
        dve_f = sem("dve_f")
        act_h = sem("act_h")
        dve_h = sem("dve_h")
        pe_d = sem("pe_d")
        dve_a = sem("dve_a")

        y_v = y.rearrange("(c j p) d -> p c j d", p=P, j=TT)
        x2_v = x2.rearrange("(c j p) d -> p c j d", p=P, j=TT)
        acc_v = acc.rearrange("(c j p) d -> p c j d", p=P, j=TT)

        def turns(body, eng):
            body(0, 0)
            body(1, 1)
            with eng.Fori(1, TURNS // 2 - 1) as cc:
                body(2 * cc, 0)
                body(2 * cc + 1, 1)
            body(TURNS - 2, 0)
            body(TURNS - 1, 1)

        def is_last(c):
            return isinstance(c, int) and c == TURNS - 1

        block = ctx.enter_context(nc.Block())

        @block.sync
        def _(sp):
            def load_y(c, par):
                wait(sp, dve_ln, TT * (c - 1))
                sp.dma_start(yb[:, par], y_v[:, bass.ds(c, 1)].rearrange("p o j d -> p (o j) d"))\
                    .then_inc(in_yb[par], 16)

            def store_x(c, par):
                wait(sp, dve_ln, TT * (c + 1))
                sp.dma_start(x2_v[:, bass.ds(c, 1)].rearrange("p o j d -> p (o j) d"), xb[:, par])\
                    .then_inc(out_x[par], 16)

            load_y(0, 0)
            sp.dma_start(r_raw[:], router_wT.rearrange("(k p) e -> p k e", p=P)).then_inc(in_r, 16)
            load_y(1, 1)
            for r, w in enumerate((gate_T, up_T, down_T)):
                sp.dma_start(s_raw[:, r], w.rearrange("(k p) i -> p k i", p=P)).then_inc(in_s[r], 16)
            sp.dma_start(bias[:], e_bias.partition_broadcast(P)).then_inc(in_b, 16)
            sp.wait_ge(pool_c, 3)
            sp.dma_start(table.rearrange("(p n) w -> p n w", p=P), empty[:]).then_inc(out_e, 16)
            store_x(0, 0)

            def body(c, par):
                if not (isinstance(c, int) and c + 2 >= TURNS):
                    load_y(c + 2, par)
                if not is_last(c):
                    store_x(c + 1, 1 - par)
                wait(sp, dve_a, TT * (c + 1))
                sp.dma_start(acc_v[:, bass.ds(c, 1)].rearrange("p o j d -> p (o j) d"), ab[:])\
                    .then_inc(out_a, 16)

            turns(body, sp)
            for par in range(2):
                sp.wait_ge(out_x[par], 16 * (TURNS // 2))
            sp.wait_ge(out_a, 16 * TURNS)
            for par in range(2):
                sp.wait_ge(out_t[par], 16 * TT * TOPK * (TURNS // 2))

        @block.gpsimd
        def _(pool):
            pool.memset(ident[:], 0.0).then_inc(pool_c, 1)
            pool.memset(every[:], 1.0).then_inc(pool_c, 1)
            pool.memset(empty[:], NOBODY).then_inc(pool_c, 1)
            pool.wait_ge(pool_c, 2)
            pool.affine_select(out=ident[:], in_=ident[:], compare_op=ALU.not_equal, fill=1.0, base=0,
                               pattern=[[-1, P]], channel_multiplier=1).then_inc(pool_c, 1)
            pool.affine_select(out=before[:], in_=every[:], compare_op=ALU.is_gt, fill=0.0, base=0,
                               pattern=[[1, P]], channel_multiplier=-1).then_inc(pool_c, 1)
            pool.iota(iota_e[:], [[1, E]], base=0, channel_multiplier=0,
                      allow_small_or_imprecise_dtypes=True).then_inc(pool_c, 1)
            pool.iota(iota_g[:], [[1, NG]], base=0, channel_multiplier=0,
                      allow_small_or_imprecise_dtypes=True).then_inc(pool_c, 1)
            pool.iota(token[:], [[P, TT], [0, TOPK]], base=-NB, channel_multiplier=1,
                      allow_small_or_imprecise_dtypes=True).then_inc(pool_c, 1)
            pool.memset(taken[:], 0.0).then_inc(pool_c, 1)
            pool.wait_ge(pool_c, 4)
            pool.wait_ge(out_e, 16)

            def body(c, par):
                wait(pool, dve_e, c + 1)
                wait(pool, pool_i, c)
                pool.tensor_tensor(idle[:], ident[:, 0:1], ident[:, 0:1], ALU.mult).then_inc(pool_i, 1)
                for j in range(TT):
                    for k in range(TOPK):
                        pool.indirect_dma_start(
                            table, bass.IndirectOffsetOnAxis(slot[:, par, j, k:k + 1], 0), entry[:, par, j, k], None,
                            bounds_check=C_SLOTS * E - 1, oob_is_err=False).then_inc(out_t[par], 16)

            turns(body, pool)

        @block.scalar
        def _(act):
            act.wait_ge(in_r, 16)
            act.copy(r_sb[:, HI], r_raw[:]).then_inc(act_s, 1)

            def hi_t(c, par, j):
                wait(act, pe_t, TT * c + j + 1)
                if j == 0:
                    wait(act, pe_f, IC * (c - 1))
                act.copy(xT2[:, par, HI, :, j * P:j * P + P], p_t[:, j % 2]).then_inc(act_t, 1)

            def sigmoid_r(c):
                wait(act, pe_r, c + 1)
                wait(act, dve_m, c)
                act.activation(prob[:].rearrange("p t e -> p (t e)"), p_r[:, 0:TT * E], ACT.Sigmoid)\
                    .then_inc(act_r, 1)

            for j in range(TT):
                hi_t(0, 0, j)
            for r in range(3):
                act.wait_ge(in_s[r], 16)
                act.copy(s_sb[:, HI, r], s_raw[:, r]).then_inc(act_s, 1)
            sigmoid_r(0)

            def body(c, par):
                for f in range(IC):
                    wait(act, pe_f, IC * c + f + 1)
                    if f < 2:
                        wait(act, dve_f1, IC * c + f - 1)
                    act.activation(sg[:, f % 2], p_f[:, f % 2, 0], ACT.Sigmoid).then_inc(act_f, 1)
                    wait(act, dve_f, IC * c + f + 1)
                    if f == 0:
                        wait(act, pe_d, TT * c)
                    act.copy(hb[:, HI, f], hf[:, f % 2]).then_inc(act_h, 1)
                    if f in (1, 2) and not is_last(c):
                        hi_t(c + 1, 1 - par, 2 * f - 2)
                        hi_t(c + 1, 1 - par, 2 * f - 1)
                if not is_last(c):
                    sigmoid_r(c + 1)

            turns(body, act)

        @block.vector
        def _(dve):
            ln = Chain(dve, ln_c, LN_LINKS)
            ro = Chain(dve, ro_c, 46)

            def norm(c, par):
                ln.turn(c)
                wait(dve, in_yb[par], 16 * ((c >> 1) + 1))
                wait(dve, out_x[par], 16 * (c >> 1))
                wait(dve, pe_t, TT * (c - 1))
                for ins in layernorm4(dve, ln, 1e-5, yb[:, par], xb[:, par], bn, mv, small, spare[:]):
                    ins.then_inc(dve_ln, 1)
                ln.close()

            def lo_t(c, par, j):
                wait(dve, act_t, TT * c + j + 1)
                at = slice(j * P, j * P + P)
                dve.tensor_tensor(xT2[:, par, LO, :, at], p_t[:, j % 2], rounded(xT2[:, par, HI, :, at]),
                                  ALU.subtract).then_inc(dve_t, 1)

            def choose_groups(c, par):
                ro.turn(c)
                tt = dve.tensor_tensor
                wait(dve, act_r, c + 1)
                wait(dve, pe_c, c)
                wait(dve, out_t[par], 16 * TT * TOPK * (c >> 1))
                ro.step(tt(sc[:], prob[:], bias[:].unsqueeze(1).to_broadcast([P, TT, E]), ALU.add))
                quad = sc[:].rearrange("p t (g q i) -> p (t g) q i", q=2, i=2)
                ro.then(tt(pair_hi[:], quad[:, :, :, 0], quad[:, :, :, 1], ALU.max))
                ro.step(tt(pair_lo[:], quad[:, :, :, 0], quad[:, :, :, 1], ALU.min))
                ro.then(tt(top1[:], pair_hi[:, :, 0], pair_hi[:, :, 1], ALU.max))
                ro.then(tt(top2[:], pair_hi[:, :, 0], pair_hi[:, :, 1], ALU.min))
                ro.step(tt(top2b[:], pair_lo[:, :, 0], pair_lo[:, :, 1], ALU.max))
                ro.step(tt(top2[:], top2[:], top2b[:], ALU.max))
                ro.then(tt(gscore[:].rearrange("p t g -> p (t g)"), top1[:], top2[:], ALU.add))
                ro.settle_idle(spare[:])
                for j in range(TT):
                    ro.then(dve.max(g8[:, j], gscore[:, j]))
                ro.settle_idle(spare[:])
                for j in range(TT):
                    ro.then(dve.max_index(gi[:, j], g8[:, j], gscore[:, j]))
                ro.settle()

            def choose_experts(c, par):
                tt = dve.tensor_tensor
                ro.step(tt(g_hot[:], gi[:, :, 0:TKG].unsqueeze(3).to_broadcast([P, TT, TKG, NG]),
                           iota_g[:].unsqueeze(1).unsqueeze(1).to_broadcast([P, TT, TKG, NG]), ALU.is_equal))
                ro.step(dve.tensor_reduce(g_mask[:], g_hot[:].rearrange("p t k g -> p t g k"), AX_X, ALU.max))
                ro.then(tt(masked[:].rearrange("p t (g i) -> p (t g) i", i=GE),
                           sc[:].rearrange("p t (g i) -> p (t g) i", i=GE),
                           g_mask[:].rearrange("p t g -> p (t g)").unsqueeze(2).to_broadcast([P, TT * NG, GE]),
                           ALU.mult))
                ro.settle_idle(spare[:])
                for j in range(TT):
                    ro.then(dve.max(e8[:, j], masked[:, j]))
                ro.settle_idle(spare[:])
                for j in range(TT):
                    ro.then(dve.max_index(ei[:, j], e8[:, j], masked[:, j]))
                ro.settle()

            def weigh(c, par):
                tt, ts = dve.tensor_tensor, dve.tensor_scalar
                ro.step(tt(hot[:], ei[:, :, 0:TOPK].unsqueeze(3).to_broadcast([P, TT, TOPK, E]),
                           iota_e[:].unsqueeze(1).unsqueeze(1).to_broadcast([P, TT, TOPK, E]), ALU.is_equal))
                ro.then(dve.tensor_reduce(chosen[:], hot[:].rearrange("p t k e -> p t e k"), AX_X, ALU.max))
                ro.step(tt(tmp[:], hot[:], prob[:].unsqueeze(2).to_broadcast([P, TT, TOPK, E]), ALU.mult))
                ro.step(dve.tensor_reduce(wk[:], tmp[:], AX_X, ALU.add))
                dve.nop().then_inc(dve_m, 1)
                ro.step(dve.tensor_reduce(wsum[:], wk[:], AX_X, ALU.add))
                ro.step(ts(winv[:], wsum[:], 1e-20, None, ALU.add))
                ro.step(dve.reciprocal(wsum[:], winv[:]))
                ro.step(tt(wk[:], wk[:], wsum[:].unsqueeze(2).to_broadcast([P, TT, TOPK]), ALU.mult))
                ro.then(ts(entry[:, par, :, :, 1], wk[:], ROUTED, None, ALU.mult))
                ro.step(ts(token[:], token[:], float(NB), None, ALU.add))
                ro.then(dve.tensor_copy(entry[:, par, :, :, 0], token[:]))

            def place(c, par):
                tt, ts, stt = dve.tensor_tensor, dve.tensor_scalar, dve.scalar_tensor_tensor
                counts = p_c[:, 0:(TT + 1) * E].rearrange("p (t e) -> p t e", e=E)
                wait(dve, pe_c, c + 1)
                ro.step(tt(pos[:], counts[:, 0:TT], taken[:].unsqueeze(1).to_broadcast([P, TT, E]), ALU.add))
                ro.then(tt(taken[:], taken[:], counts[:, TT], ALU.add))
                ro.step(tt(tmp[:], hot[:], pos[:].unsqueeze(2).to_broadcast([P, TT, TOPK, E]), ALU.mult))
                ro.step(dve.tensor_reduce(pos_k[:], tmp[:], AX_X, ALU.add))
                ro.then(ts(second[:], pos_k[:], float(HALF), None, ALU.is_ge))
                ro.step(ts(column[:], ei[:, :, 0:TOPK], 2.0, None, ALU.mult))
                ro.step(stt(out=column[:], in0=second[:], scalar=float(1 - HALF * COLS), in1=column[:],
                            op0=ALU.mult, op1=ALU.add))
                ro.step(stt(out=slot[:, par], in0=pos_k[:], scalar=float(COLS), in1=column[:],
                            op0=ALU.mult, op1=ALU.add))
                dve.nop().then_inc(dve_e, 1)
                ro.close()

            def hidden(c, f):
                wait(dve, act_f, IC * c + f + 1)
                dve.tensor_tensor(hf[:, f % 2], sg[:, f % 2], p_f[:, f % 2, 0], ALU.mult).then_inc(dve_f1, 1)
                wait(dve, dve_f1, IC * c + f + 1)
                dve.tensor_tensor(hf[:, f % 2], hf[:, f % 2], p_f[:, f % 2, 1], ALU.mult).then_inc(dve_f, 1)
                wait(dve, act_h, IC * c + f + 1)
                dve.tensor_tensor(hb[:, LO, f], hf[:, f % 2], rounded(hb[:, HI, f]), ALU.subtract)\
                    .then_inc(dve_h, 1)

            dve.wait_ge(act_s, 1)
            dve.tensor_tensor(r_sb[:, LO], r_raw[:], rounded(r_sb[:, HI]), ALU.subtract).then_inc(dve_s, 1)
            norm(0, 0)
            for j in range(TT):
                lo_t(0, 0, j)
            for r in range(3):
                dve.wait_ge(act_s, 2 + r)
                dve.tensor_tensor(s_sb[:, LO, r], s_raw[:, r], rounded(s_sb[:, HI, r]), ALU.subtract)\
                    .then_inc(dve_s, 1)
            dve.wait_ge(pool_c, 9)
            dve.wait_ge(in_b, 16)

            def body(c, par):
                if is_last(c):
                    choose_groups(c, par)
                    choose_experts(c, par)
                    weigh(c, par)
                    hidden(c, 0)
                    place(c, par)
                    hidden(c, 1)
                    hidden(c, 2)
                    hidden(c, 3)
                else:
                    norm(c + 1, 1 - par)
                    hidden(c, 0)
                    choose_groups(c, par)
                    hidden(c, 1)
                    lo_t(c + 1, 1 - par, 0)
                    lo_t(c + 1, 1 - par, 1)
                    choose_experts(c, par)
                    hidden(c, 2)
                    lo_t(c + 1, 1 - par, 2)
                    lo_t(c + 1, 1 - par, 3)
                    weigh(c, par)
                    hidden(c, 3)
                wait(dve, out_a, 16 * c)
                for j in range(TT):
                    wait(dve, pe_d, TT * c + j + 1)
                    dve.tensor_tensor(ab[:, j], xb[:, par, j], p_f[:, j // 2, j % 2], ALU.add)\
                        .then_inc(dve_a, 1)
                    if j == 1 and not is_last(c):
                        place(c, par)

            turns(body, dve)

        @block.tensor
        def _(pe):
            def turn(c, par, j):
                wait(pe, dve_ln, TT * c + j + 1)
                wait(pe, dve_t, TT * c + j - 1)
                for k in range(KC):
                    ins = pe.transpose(p_t[:, j % 2, k], xb[:, par, j, k * P:k * P + P], ident[:])
                ins.then_inc(pe_t, 1)

            def logits(c, par):
                wait(pe, dve_t, TT * (c + 1))
                wait(pe, act_r, c)
                for j in range(TT):
                    for k in range(KC):
                        for a, b in PASSES:
                            ins = pe.matmul(p_r[:, j * E:j * E + E], xT2[:, par, a, k, j * P:j * P + P],
                                            r_sb[:, b, k], start=(k == 0 and (a, b) == PASSES[0]),
                                            stop=(k == KC - 1 and (a, b) == PASSES[-1]))
                ins.then_inc(pe_r, 1)

            def count(c):
                wait(pe, dve_m, c + 1)
                wait(pe, dve_e, c)
                for j in range(TT + 1):
                    out = p_c[:, j * E:j * E + E]
                    for i in range(min(j, TT)):
                        ins = pe.matmul(out, every[:], chosen[:, i], start=(i == 0),
                                        stop=(j == TT and i == TT - 1))
                    if j < TT:
                        ins = pe.matmul(out, before[:], chosen[:, j], start=(j == 0), stop=True)
                ins.then_inc(pe_c, 1)

            def gate_up(c, par, f):
                if f < 2:
                    wait(pe, dve_a, TT * (c - 1) + 2 * f + 2)
                else:
                    wait(pe, dve_f, IC * c + f - 1)
                for r in range(2):
                    for k in range(KC):
                        for a, b in PASSES:
                            ins = pe.matmul(p_f[:, f % 2, r], s_sb[:, a, r, k, f * P:f * P + P],
                                            xT2[:, par, b, k], start=(k == 0 and (a, b) == PASSES[0]),
                                            stop=(k == KC - 1 and (a, b) == PASSES[-1]))
                ins.then_inc(pe_f, 1)

            def down(c, j):
                if j == 0:
                    wait(pe, dve_h, IC * (c + 1))
                for k in range(IC):
                    for a, b in PASSES:
                        ins = pe.matmul(p_f[:, j // 2, j % 2], hb[:, a, k, j * P:j * P + P], s_sb[:, b, 2, k],
                                        start=(k == 0 and (a, b) == PASSES[0]),
                                        stop=(k == IC - 1 and (a, b) == PASSES[-1]))
                ins.then_inc(pe_d, 1)

            pe.wait_ge(pool_c, 9)
            for j in range(TT):
                turn(0, 0, j)
            pe.wait_ge(dve_s, 1)
            logits(0, 0)
            pe.wait_ge(dve_s, 3)

            def body(c, par):
                for f in range(IC):
                    gate_up(c, par, f)
                    if f in (1, 2) and not is_last(c):
                        turn(c + 1, 1 - par, 2 * f - 2)
                        turn(c + 1, 1 - par, 2 * f - 1)
                    if f == 1 and is_last(c):
                        count(c)
                if not is_last(c):
                    logits(c + 1, 1 - par)
                if isinstance(c, int) and c == 0:
                    pe.wait_ge(dve_s, 4)
                for j in range(TT):
                    down(c, j)
                    if j == 1 and not is_last(c):
                        count(c)

            turns(body, pe)


def experts(nc, ident, x2, acc, table, w_gate, w_up, w_down, C_SLOTS):
    E, D, I = w_gate.shape
    N = x2.shape[0]
    KC, IC = D // P, I // P
    HALF = C_SLOTS // 2
    COLS = 2 * E
    assert KC == 4 and IC == 2

    with ExitStack() as ctx:
        def sb(name, shape, dt=F32):
            return ctx.enter_context(nc.sbuf_tensor(name, shape, dt))

        def ps(name, shape):
            return ctx.enter_context(nc.psum_tensor(name, shape, F32))

        def sem(name):
            return ctx.enter_context(nc.semaphore(name))

        def rounded(tile):
            return tile.bitcast(F32)

        GU = 2 * KC * I
        w_raw = sb("ew_raw", [P, 2, GU + IC * D])
        w_sb = sb("ew_sb", [P, 2, 2, GU + IC * D], F32R)
        slots = sb("slots", [HALF, COLS, 2])
        who = sb("who", [HALF, 2, 2], U32)
        to = sb("to", [HALF, 2, 2], U32)
        weight = sb("weight", [HALF, 2, 2])
        xg = sb("xg", [HALF, 2, 2, D])
        xT = sb("exT", [P, 2, 2, KC, C_SLOTS], F32R)
        sg = sb("esg", [P, 2, IC * C_SLOTS])
        hf = sb("ehf", [P, 2, IC * C_SLOTS])
        hb = sb("ehb", [P, 2, 2, IC * C_SLOTS], F32R)
        yo = sb("yo", [HALF, 2, 2, D])
        idle = sb("eidle", [P, 2])

        p_t = ps("ep_t", [P, 2, NB])
        p_f = ps("ep_f", [P, 2, 2, NB])
        p_y = ps("ep_y", [P, 2, NB])

        in_w = [[sem(f"in_ew{q}{r}") for r in range(3)] for q in range(2)]
        in_t = sem("in_t")
        in_x = [[sem(f"in_ex{q}{h}") for h in range(2)] for q in range(2)]
        out_y = [sem(f"out_ey{h}") for h in range(2)]
        dve_x = sem("dve_ex")
        pool_i = [sem(f"pool_ei{q}") for q in range(2)]
        act_wg = sem("act_wg")
        act_wd = sem("act_wd")
        dve_w = sem("dve_ew")
        pool_w = sem("pool_ew")
        dve_i = sem("dve_i")
        dve_o = sem("dve_o")
        pe_t = sem("pe_et")
        act_t = sem("act_et")
        dve_t = sem("dve_et")
        pe_f = sem("pe_ef")
        act_f = sem("act_ef")
        dve_f1 = sem("dve_ef1")
        dve_f = sem("dve_ef")
        act_h = sem("act_eh")
        dve_h = sem("dve_eh")
        pe_y = sem("pe_ey")
        act_y = sem("act_ey")

        def gate_up_of(par, part=None):
            t = w_raw[:, par, 0:GU] if part is None else w_sb[:, par, part, 0:GU]
            return t.rearrange("p (r k i) -> p r k i", r=2, k=KC)

        def down_of(par, part=None):
            t = w_raw[:, par, GU:] if part is None else w_sb[:, par, part, GU:]
            return t.rearrange("p (k d) -> p k d", k=IC)

        g_dram = w_gate.rearrange("e (k p) i -> p e k i", p=P)
        u_dram = w_up.rearrange("e (k p) i -> p e k i", p=P)
        d_dram = w_down.rearrange("e (k p) d -> p e k d", p=P)

        def by_pairs(eng, body):
            def two(e):
                body(e, 0)
                body(e + 1, 1)
            two(0)
            with eng.Fori(1, E // 2 - 2) as ee:
                two(2 * ee)
            two(E - 4)
            two(E - 2)

        def there(e):
            return not (isinstance(e, int) and e >= E)

        block = ctx.enter_context(nc.Block())


        @block.sync
        def _(sp):
            sp.dma_start(slots[:], table.rearrange("(p n) w -> p n w", p=HALF)).then_inc(in_t, 16)

            def load(e, par):
                wait(sp, act_wg, e - 1)
                wait(sp, dve_w, e - 1)
                for r, src in enumerate((g_dram, u_dram)):
                    sp.dma_start(gate_up_of(par)[:, r], src[:, bass.ds(e, 1)].rearrange("p o k i -> p (o k) i"))\
                        .then_inc(in_w[par][r], 16)
                wait(sp, act_wd, e - 1)
                wait(sp, pool_w, e - 1)
                sp.dma_start(down_of(par), d_dram[:, bass.ds(e, 1)].rearrange("p o k d -> p (o k) d"))\
                    .then_inc(in_w[par][2], 16)

            by_pairs(sp, load)
            for h in range(2):
                sp.wait_ge(out_y[h], 16 * E)

        @block.gpsimd
        def _(pool):
            pool.wait_ge(dve_x, 1)

            def carry(q, before):
                wait(pool, pool_i[q], before)
                pool.tensor_tensor(idle[:, q:q + 1], ident[:, 0:1], ident[:, 0:1], ALU.mult)\
                    .then_inc(pool_i[q], 1)

            def gather(e, par):
                wait(pool, dve_i, e + 1)
                wait(pool, pe_t, 2 * (e - 1))
                carry(0, e)
                for h in range(2):
                    pool.indirect_dma_start(xg[:, par, h], None, x2,
                                            bass.IndirectOffsetOnAxis(who[:, par, h:h + 1], 0),
                                            bounds_check=N - 1, oob_is_err=False).then_inc(in_x[par][h], 16)

            def lo_down(e, par):
                wait(pool, act_wd, e + 1)
                pool.tensor_tensor(down_of(par, LO), down_of(par), rounded(down_of(par, HI)), ALU.subtract)\
                    .then_inc(pool_w, 1)

            def add(e, par):
                wait(pool, dve_o, e + 1)
                for h in range(2):
                    wait(pool, act_y, 2 * e + h + 1)
                    for g in range(2):
                        wait(pool, out_y[g], 16 * e)
                    carry(1, 2 * e + h)
                    pool.indirect_dma_start(acc, bass.IndirectOffsetOnAxis(to[:, par, h:h + 1], 0),
                                            yo[:, par, h], None, bounds_check=N - 1, oob_is_err=False,
                                            compute_op=ALU.add).then_inc(out_y[h], 16)

            def body(e, par):
                if there(e + 3):
                    gather(e + 3, 1 - par)
                if there(e + 1):
                    lo_down(e + 1, 1 - par)
                add(e, par)

            gather(0, 0)
            gather(1, 1)
            lo_down(0, 0)
            gather(2, 0)
            by_pairs(pool, body)

        @block.scalar
        def _(act):
            def hi_gate_up(e, par):
                for r in range(2):
                    wait(act, in_w[par][r], 16 * ((e >> 1) + 1))
                wait(act, pe_f, e - 1)
                act.copy(gate_up_of(par, HI), gate_up_of(par)).then_inc(act_wg, 1)

            def hi_down(e, par):
                wait(act, in_w[par][2], 16 * ((e >> 1) + 1))
                wait(act, pe_y, 2 * (e - 1))
                act.copy(down_of(par, HI), down_of(par)).then_inc(act_wd, 1)

            def hi_x(e, par):
                for b in range(2):
                    wait(act, pe_t, 2 * e + b + 1)
                    if b == 0:
                        wait(act, pe_f, e - 1)
                    act.copy(xT[:, par, HI, 2 * b:2 * b + 2].rearrange("p k s -> p (k s)"),
                             p_t[:, b, 0:2 * C_SLOTS]).then_inc(act_t, 1)

            def sigmoid(e, par):
                wait(act, pe_f, e + 1)
                act.activation(sg[:, par], p_f[:, par, 0, 0:IC * C_SLOTS], ACT.Sigmoid).then_inc(act_f, 1)

            def hi_h(e, par):
                wait(act, dve_f, e + 1)
                wait(act, pe_y, 2 * (e - 1))
                act.copy(hb[:, par, HI], hf[:, par]).then_inc(act_h, 1)

            def weigh(e, par):
                wait(act, dve_o, e + 1)
                for h in range(2):
                    wait(act, pe_y, 2 * e + h + 1)
                    wait(act, out_y[h], 16 * (e - 1))
                    act.activation(yo[:, par, h], p_y[0:HALF, h], ACT.Copy, scale=weight[:, par, h:h + 1])\
                        .then_inc(act_y, 1)

            def body(e, par):
                if there(e + 2):
                    hi_gate_up(e + 2, par)
                    hi_x(e + 2, par)
                if there(e + 1):
                    hi_down(e + 1, 1 - par)
                    sigmoid(e + 1, 1 - par)
                    hi_h(e + 1, 1 - par)
                weigh(e, par)

            hi_gate_up(0, 0)
            hi_x(0, 0)
            hi_gate_up(1, 1)
            sigmoid(0, 0)
            hi_down(0, 0)
            hi_h(0, 0)
            hi_x(1, 1)
            by_pairs(act, body)

        @block.vector
        def _(dve):
            def fetch(e, par):
                for h in range(2):
                    wait(dve, in_x[par][h], 16 * (e >> 1))
                dve.tensor_copy(who[:, par], slots[:, bass.ds(2 * e, 2), 0]).then_inc(dve_i, 1)

            def ready(e, par):
                for h in range(2):
                    wait(dve, out_y[h], 16 * (e - 1))
                wait(dve, act_y, 2 * (e - 1))
                dve.tensor_copy(to[:, par], slots[:, bass.ds(2 * e, 2), 0])
                dve.tensor_copy(weight[:, par], slots[:, bass.ds(2 * e, 2), 1]).then_inc(dve_o, 1)

            def lo_gate_up(e, par):
                wait(dve, act_wg, e + 1)
                dve.tensor_tensor(gate_up_of(par, LO), gate_up_of(par), rounded(gate_up_of(par, HI)),
                                  ALU.subtract).then_inc(dve_w, 1)

            def lo_x(e, par):
                for b in range(2):
                    wait(dve, act_t, 2 * e + b + 1)
                    two = xT[:, par, :, 2 * b:2 * b + 2].rearrange("p a k s -> p a (k s)")
                    dve.tensor_tensor(two[:, LO], p_t[:, b, 0:2 * C_SLOTS], rounded(two[:, HI]),
                                      ALU.subtract).then_inc(dve_t, 1)

            def hidden(e, par):
                wait(dve, act_f, e + 1)
                dve.tensor_tensor(hf[:, par], sg[:, par], p_f[:, par, 0, 0:IC * C_SLOTS], ALU.mult)\
                    .then_inc(dve_f1, 1)
                wait(dve, dve_f1, e + 1)
                dve.tensor_tensor(hf[:, par], hf[:, par], p_f[:, par, 1, 0:IC * C_SLOTS], ALU.mult)\
                    .then_inc(dve_f, 1)
                wait(dve, act_h, e + 1)
                dve.tensor_tensor(hb[:, par, LO], hf[:, par], rounded(hb[:, par, HI]), ALU.subtract)\
                    .then_inc(dve_h, 1)

            def body(e, par):
                ready(e, par)
                if there(e + 2):
                    lo_gate_up(e + 2, par)
                    lo_x(e + 2, par)
                if there(e + 1):
                    hidden(e + 1, 1 - par)
                if there(e + 4):
                    fetch(e + 4, par)

            dve.memset(xg[:], 0.0).then_inc(dve_x, 1)
            dve.wait_ge(in_t, 16)
            fetch(0, 0)
            fetch(1, 1)
            lo_gate_up(0, 0)
            lo_x(0, 0)
            lo_gate_up(1, 1)
            fetch(2, 0)
            hidden(0, 0)
            lo_x(1, 1)
            fetch(3, 1)
            by_pairs(dve, body)

        @block.tensor
        def _(pe):
            def transposes(e, par):
                for h in range(2):
                    wait(pe, in_x[par][h], 16 * ((e >> 1) + 1))
                for b in range(2):
                    wait(pe, dve_t, 2 * (e - 1) + b + 1)
                    for k in range(2 * b, 2 * b + 2):
                        for h in range(2):
                            at = (k % 2) * C_SLOTS + h * HALF
                            ins = pe.transpose(p_t[:, b, at:at + HALF], xg[:, par, h, k * P:k * P + P],
                                               ident[0:HALF, 0:HALF])
                    ins.then_inc(pe_t, 1)

            def gate_up(e, par):
                wait(pe, dve_w, e + 1)
                wait(pe, dve_t, 2 * (e + 1))
                wait(pe, dve_f, e - 1)
                for r in range(2):
                    for ic in range(IC):
                        for k in range(KC):
                            for a, b in PASSES:
                                w = gate_up_of(par, a)[:, r, k, ic * P:ic * P + P]
                                ins = pe.matmul(p_f[:, par, r, ic * C_SLOTS:(ic + 1) * C_SLOTS], w,
                                                xT[:, par, b, k], start=(k == 0 and (a, b) == PASSES[0]),
                                                stop=(k == KC - 1 and (a, b) == PASSES[-1]))
                ins.then_inc(pe_f, 1)

            def down(e, par):
                wait(pe, pool_w, e + 1)
                wait(pe, dve_h, e + 1)
                for h in range(2):
                    wait(pe, act_y, 2 * (e - 1) + h + 1)
                    for ic in range(IC):
                        at = ic * C_SLOTS + h * HALF
                        for a, b in PASSES:
                            ins = pe.matmul(p_y[0:HALF, h], hb[:, par, a, at:at + HALF], down_of(par, b)[:, ic],
                                            start=(ic == 0 and (a, b) == PASSES[0]),
                                            stop=(ic == IC - 1 and (a, b) == PASSES[-1]))
                    ins.then_inc(pe_y, 1)

            def body(e, par):
                if there(e + 2):
                    transposes(e + 2, par)
                if there(e + 1):
                    gate_up(e + 1, 1 - par)
                down(e, par)

            transposes(0, 0)
            gate_up(0, 0)
            transposes(1, 1)
            by_pairs(pe, body)


def last_norm(nc, acc, out):
    N, D = acc.shape
    TT = NB // P
    TURNS = N // NB
    with ExitStack() as ctx:
        def sb(name, shape, dt=F32):
            return ctx.enter_context(nc.sbuf_tensor(name, shape, dt))

        a_in = sb("a_in", [P, 2, TT, D])
        a_out = sb("a_out", [P, 2, TT, D])
        bn = sb("lbn", [P, TT, 6])
        mv = sb("lmv", [P, TT, 2])
        small = sb("lsmall", [P, 3, TT])
        spare = sb("lspare", [P, 1])
        loaded = [ctx.enter_context(nc.semaphore(f"l_in{q}")) for q in range(2)]
        stored = [ctx.enter_context(nc.semaphore(f"l_out{q}")) for q in range(2)]
        ln_c = ctx.enter_context(nc.semaphore("l_c"))
        dve_o = ctx.enter_context(nc.semaphore("l_o"))

        acc_v = acc.rearrange("(c j p) d -> p c j d", p=P, j=TT)
        out_v = out.rearrange("b s d -> (b s) d").rearrange("(c j p) d -> p c j d", p=P, j=TT)
        block = ctx.enter_context(nc.Block())

        def turns(eng, body):
            body(0, 0)
            body(1, 1)
            with eng.Fori(1, TURNS // 2) as g:
                body(2 * g, 0)
                body(2 * g + 1, 1)

        @block.sync
        def _(sp):
            def load(c, q):
                wait(sp, dve_o, TT * (c - 1))
                sp.dma_start(a_in[:, q], acc_v[:, bass.ds(c, 1)].rearrange("p o j d -> p (o j) d"))\
                    .then_inc(loaded[q], 16)

            turns(sp, load)

        @block.scalar
        def _(act):
            def store(c, q):
                wait(act, dve_o, TT * (c + 1))
                act.dma_start(out_v[:, bass.ds(c, 1)].rearrange("p o j d -> p (o j) d"), a_out[:, q])\
                    .then_inc(stored[q], 16)

            turns(act, store)
            for q in range(2):
                act.wait_ge(stored[q], 16 * (TURNS // 2))

        @block.vector
        def _(dve):
            link = Chain(dve, ln_c, LN_LINKS)

            def norm(c, q):
                link.turn(c)
                wait(dve, loaded[q], 16 * ((c >> 1) + 1))
                wait(dve, stored[q], 16 * (c >> 1))
                for ins in layernorm4(dve, link, 1e-5, a_in[:, q], a_out[:, q], bn, mv, small, spare[:]):
                    ins.then_inc(dve_o, 1)
                link.close()

            turns(dve, norm)


N_EXPERTS_FACTOR = (5, 4)


def build(nc, x, xT, w_qkv, w_o, router_wT, e_bias, w_gate, w_up, w_down, gate_T, up_T, down_T, out):
    B, S, D = x.shape
    N, E = B * S, w_gate.shape[0]
    a, b = N_EXPERTS_FACTOR
    c_slots = -(-a * N // (b * E))

    def scratch(name, shape):
        return nc.dram_tensor(name, shape, F32, kind="Internal").ap()

    y, x2, acc = (scratch(n, (N, D)) for n in ("y_rows", "x2_rows", "acc_rows"))
    table = scratch("slot_table", (E * c_slots, 2))
    attention(nc, x, xT, w_qkv, w_o, y)
    with nc.sbuf_tensor("ident", [P, P], F32) as ident:
        route_and_share(nc, ident, y, router_wT, e_bias, gate_T, up_T, down_T, x2, acc, table, c_slots)
        experts(nc, ident, x2, acc, table, w_gate, w_up, w_down, c_slots)
    last_norm(nc, acc, out)


def kernel(**inputs):
    import numpy as _np
    import concourse.bacc as _bacc
    from concourse import mybir as _mybir
    from concourse.bass_utils import run_bass_kernel_spmd as _run

    nc = _bacc.Bacc("TRN2", target_bir_lowering=False, num_devices=1)
    given = {k: _np.asarray(v) for k, v in inputs.items()}
    x = given["L0_attn_x"]
    laid_out = {
        "x": x,
        "xT": x.reshape(-1, x.shape[-1]).T,
        "w_qkv": given["L0_attn_w_qkv"],
        "w_o": given["L0_attn_w_o"],
        "router_wT": given["L0_ffn_router_w"].T,
        "e_bias": given["L0_ffn_e_bias"],
        "w_gate": given["L0_ffn_W_gate"],
        "w_up": given["L0_ffn_W_up"],
        "w_down": given["L0_ffn_W_down"],
        "gate_T": given["L0_ffn_shared_gate"].T,
        "up_T": given["L0_ffn_shared_up"].T,
        "down_T": given["L0_ffn_shared_down"].T,
    }
    arrays, args = {}, []
    for name, a in laid_out.items():
        a = _np.ascontiguousarray(a)
        arrays[f"in_{name}"] = a
        args.append(nc.dram_tensor(f"in_{name}", a.shape, _mybir.dt.from_np(a.dtype), kind="ExternalInput").ap())
    args.append(nc.dram_tensor("out_rows", x.shape, F32, kind="ExternalOutput").ap())
    build(nc, *args)
    r = _run(nc, [arrays], core_ids=[0])
    return r.results[0]["out_rows"]
```

```python
from contextlib import ExitStack

import concourse.bass as bass
from concourse import mybir

F32 = mybir.dt.float32
F32R = mybir.dt.float32r
U32 = mybir.dt.uint32
BF16 = mybir.dt.bfloat16
ALU = mybir.AluOpType
ACT = mybir.ActivationFunctionType
AX_X = mybir.AxisListType.X

P = 128
NB = 512
HI, LO = 0, 1
PASSES = ((HI, HI), (HI, LO), (LO, HI))


def wait(eng, sem, value):
    if not (isinstance(value, int) and value <= 0):
        eng.wait_ge(sem, value)


def attention(nc, norm1, x, xT, w_qkv, w_o, y):
    B, S, D = x.shape
    F = w_o.shape[0]
    DH = 128
    H = F // DH
    M = B * H
    C = D // P
    T = S // P
    HALVES = S // NB
    PAIRS = M // 2
    PB = H // 2
    SCALE = float(DH) ** -0.5
    Q, K, V = range(3)
    G = 3 * HALVES
    assert T == 8 and HALVES == 2 and PB == T and C == 4

    with ExitStack() as ctx:
        def sb(name, shape, dt=F32):
            return ctx.enter_context(nc.sbuf_tensor(name, shape, dt))

        def sem(name):
            return ctx.enter_context(nc.semaphore(name))

        xt = sb("xt", [P, 2, 2, C, S], F32R)
        x_raw = sb("x_raw", [P, 2, C, P])
        y_sb = sb("y_sb", [P, T, D])
        w_raw = sb("w_raw", [P, 3, C, DH])
        w_sb = sb("w_sb", [P, 2, 3, C, DH], F32R)
        wo_raw = sb("wo_raw", [P, 2, D])
        wo_sb = sb("wo_sb", [P, 2, 2, D], F32R)
        qk = sb("qk", [P, 2, 2, 2, S], F32R)
        by_two = lambda tile: tile.rearrange("p j d -> p (j d)").rearrange("p (a s) -> p a s", a=2)
        ex = by_two(norm1.y[0][:])
        colsum = sb("colsum", [P, S])
        cs = sb("cs", [P, 2, S], F32R)
        v_sb = sb("v_sb", [P, 2, S])
        val = by_two(norm1.x2[0][:])
        val2 = sb("val2", [P, 2, 2, S], F32R)
        ones_f = sb("ones_f", [P, P])
        ones = sb("ones", [P, P], F32R)
        neg_max = sb("neg_max", [P, 2, 1])
        rowsum = sb("rowsum", [P, 2, 1])
        inv = sb("inv", [P, 2, 1])
        W_AFTER = (0, T // 2 - 1, T - 3)
        first_x = [x_raw[:, k] for k in range(2)]
        for buf in (ex, val):
            first_x += [buf[:, a, b * NB:b * NB + NB].rearrange("p (c t) -> p c t", c=C)
                        for a in range(2) for b in range(HALVES)]
        p_s = ctx.enter_context(nc.psum_tensor("p_s", [P, 2, S], F32))
        p_g = ctx.enter_context(nc.psum_tensor("p_g", [P, 2, NB], F32))
        p_o = ctx.enter_context(nc.psum_tensor("p_o", [P, 2, NB], F32))

        in_w = [sem(f"in_w{r}") for r in range(3)]
        in_wo = [sem(f"in_wo{r}") for r in range(2)]
        in_first = [sem(f"in_first{k}") for k in range(T)]
        in_x = sem("in_x")
        in_y = [sem(f"in_y{j}") for j in range(T)]
        out_y = [sem(f"out_y{j}") for j in range(T)]
        pe_s = sem("pe_s")
        pe_g = sem("pe_g")
        pe_cs = sem("pe_cs")
        pe_o = sem("pe_o")
        act_e = sem("act_e")
        act_g = sem("act_g")
        act_cs = sem("act_cs")
        act_val = sem("act_val")
        act_w = sem("act_w")
        act_wo = sem("act_wo")
        act_x = sem("act_x")
        dve_m = sem("dve_m")
        dve_r = sem("dve_r")
        dve_p = sem("dve_p")
        dve_g = sem("dve_g")
        dve_cs = sem("dve_cs")
        dve_v = sem("dve_v")
        dve_val = sem("dve_val")
        dve_y = sem("dve_y")
        dve_1 = sem("dve_1")
        pool_w = sem("pool_w")
        pool_wo = sem("pool_wo")
        pool_x = sem("pool_x")

        def rounded(tile):
            return tile.bitcast(F32)

        def xt_part(par, part, c, at, size):
            whole = xt[:].rearrange("p a h c t -> p (a h c t)")
            return whole[:, bass.ds(par * (2 * C * S) + at + (part * C * S + c * S), size)]

        w_dram = w_qkv.rearrange("(c p) (r h f) -> p r h c f", p=P, r=3, f=DH)
        wo_dram = w_o.rearrange("(h p) d -> p h d", p=P)
        xT_dram = xT.rearrange("(c p) (n t) -> p n c t", p=P, t=P)
        x_rows = x.rearrange("b (j p) d -> p b j d", p=P)
        y_rows = y.rearrange("(b j p) d -> p b j d", p=P, j=T)

        block = ctx.enter_context(nc.Block())

        @block.sync
        def _(sp):
            def load_w(h, m, parts=range(3)):
                for r in parts:
                    wait(sp, act_w, 3 * (m - 1) + r + 1)
                    wait(sp, pool_w, 3 * (m - 1) + r + 1)
                    src = w_dram[:, r, bass.ds(h, 1)].rearrange("p o c f -> p (o c) f")
                    sp.dma_start(w_raw[:, r], src).then_inc(in_w[r], 16)

            def load_wo(h, m, r):
                wait(sp, act_wo, m - 1)
                wait(sp, pool_wo, m - 1)
                sp.dma_start(wo_raw[:, r], wo_dram[:, bass.ds(h, 1)].rearrange("p o d -> p (o d)"))\
                    .then_inc(in_wo[r], 16)

            def load_x(k):
                wait(sp, act_x, k)
                wait(sp, pool_x, k)
                sp.dma_start(x_raw[:, 0], xT_dram[:, bass.ds(k, 1)].rearrange("p o c t -> p (o c) t"))\
                    .then_inc(in_x, 16)

            def pair(b, k, last=False, more_x=True, first=False):
                i = b * PB + k
                for s in range(2):
                    n = 2 * i + s
                    if not last:
                        load_w((2 * k + s + 2) % H if isinstance(k, int) else 2 * k + (s + 2), n + 2)
                    load_wo(2 * k + s, n, s)
                    if s == 0 and more_x:
                        load_x(T + i)
                    if k_is(k, 0) and not first:
                        swap(b, s)

            def k_is(k, v):
                return isinstance(k, int) and k == v

            def swap(b, s):
                for j in range(4 * s, 4 * s + 4):
                    wait(sp, dve_y, (b * PB - 1) * T + j + 1)
                    store_y(b - 1, j)
                for j in range(4 * s, 4 * s + 4):
                    wait(sp, out_y[j], 16 * b)
                    load_y(b, j)

            def store_y(b, j):
                sp.dma_start(y_rows[:, bass.ds(b, 1), j].rearrange("p o d -> p (o d)"), y_sb[:, j])\
                    .then_inc(out_y[j], 16)

            def load_y(b, j):
                sp.dma_start(y_sb[:, j], x_rows[:, bass.ds(b, 1), j].rearrange("p o d -> p (o d)"))\
                    .then_inc(in_y[j], 16)

            for k in range(T):
                sp.dma_start(first_x[k], xT_dram[:, k]).then_inc(in_first[k], 16)
                if k in W_AFTER:
                    load_w(0, 0, [W_AFTER.index(k)])
            load_w(1, 1)
            for j in range(T):
                load_y(0, j)
            pair(0, 0, first=True)
            with sp.Fori(1, PB - 1) as k:
                pair(0, k)
            pair(0, PB - 1)
            with sp.Fori(1, B - 1) as b:
                pair(b, 0)
                with sp.Fori(1, PB - 1) as k:
                    pair(b, k)
                pair(b, PB - 1)
            pair(B - 1, 0, more_x=False)
            with sp.Fori(1, PB - 1) as k:
                pair(B - 1, k, more_x=False)
            pair(B - 1, PB - 1, last=True, more_x=False)
            wait(sp, dve_p, T * M)
            norm1.load(sp, y, 0, 0)
            for j in range(T):
                wait(sp, dve_y, (PAIRS - 1) * T + j + 1)
                store_y(B - 1, j)
            for j in range(T):
                wait(sp, out_y[j], 16 * B)

        def pairs(eng, pair):
            pair(0)
            pair(1)
            with eng.Fori(2, (B - 1) * PB) as i:
                pair(i)
            with eng.Fori((B - 1) * PB, PAIRS - 1) as i:
                pair(i, more_x=False)
            pair(PAIRS - 1, more_x=False)

        def is_last(i):
            return isinstance(i, int) and i == PAIRS - 1

        def is_first(i):
            return isinstance(i, int) and i == 0

        def x_piece(k):
            return (k >> 3) & 1, (k & 7) * P

        @block.gpsimd
        def _(pool):
            def lo_w(m, r):
                wait(pool, act_w, 3 * m + r + 1)
                pool.tensor_tensor(w_sb[:, LO, r], w_raw[:, r], rounded(w_sb[:, HI, r]), ALU.subtract)\
                    .then_inc(pool_w, 1)

            def lo_wo(m, r):
                wait(pool, act_wo, m + 1)
                pool.tensor_tensor(wo_sb[:, r, LO], wo_raw[:, r], rounded(wo_sb[:, r, HI]), ALU.subtract)\
                    .then_inc(pool_wo, 1)

            def lo_x(k):
                wait(pool, act_x, k + 1)
                par, at = x_piece(k)
                for c in range(C):
                    ins = pool.tensor_tensor(xt_part(par, LO, c, at, P), x_raw[:, 0, c],
                                             rounded(xt_part(par, HI, c, at, P)), ALU.subtract)
                ins.then_inc(pool_x, 1)

            def pair(i, more_x=True):
                for s in range(2):
                    n = 2 * i + s
                    if s == 0 and not is_first(i):
                        lo_wo(n - 2, 0)
                    if not is_last(i):
                        lo_w(n + 2, Q)
                    if s == 0 and not is_first(i):
                        lo_wo(n - 1, 1)
                    if not is_last(i):
                        lo_w(n + 2, K)
                    if s == 0 and more_x:
                        lo_x(T + i)
                    if not is_last(i):
                        lo_w(n + 2, V)

            for m in range(2):
                for r in range(3):
                    lo_w(m, r)
            pairs(pool, pair)
            lo_wo(M - 2, 0)
            lo_wo(M - 1, 1)

        @block.scalar
        def _(act):
            def hi_w(m, r):
                wait(act, in_w[r], 16 * (m + 1))
                wait(act, pe_g, G * (m - 1) + 2 * r + 2)
                act.copy(w_sb[:, HI, r], w_raw[:, r]).then_inc(act_w, 1)

            def hi_wo(m, r, i):
                wait(act, in_wo[r], 16 * i)
                wait(act, pe_o, T * (i - 1))
                act.copy(wo_sb[:, r, HI], wo_raw[:, r]).then_inc(act_wo, 1)

            def hi_x(k, heads):
                wait(act, in_x, 16 * (k - T + 1))
                wait(act, pe_g, G * heads)
                par, at = x_piece(k)
                for c in range(C):
                    ins = act.copy(xt_part(par, HI, c, at, P), x_raw[:, 0, c])
                ins.then_inc(act_x, 1)

            def hi_g(m, par, g):
                r, half = divmod(g, 2)
                at = slice(half * NB, half * NB + NB)
                wait(act, pe_g, G * m + g + 1)
                if r == V:
                    if g == 4:
                        wait(act, dve_v, 2 * (m - 1))
                    act.copy(v_sb[:, par, at], p_g[:, g % 2]).then_inc(act_g, 1)
                else:
                    if g == 0:
                        wait(act, pe_s, T * (m - 1))
                    act.activation(qk[:, par, r, HI, at], p_g[:, g % 2], ACT.Copy,
                                   scale=SCALE if r == Q else 1.0).then_inc(act_g, 1)

            def hi_cs(m):
                wait(act, dve_p, T * (m + 1))
                wait(act, pe_cs, 2 * m)
                act.copy(cs[:, HI], colsum[:]).then_inc(act_cs, 1)

            def hi_val(m, r, i):
                wait(act, dve_v, 2 * (m + 1))
                wait(act, pe_o, T * (i - 1))
                act.copy(val2[:, r, HI], val[:, r]).then_inc(act_val, 1)

            def exp_tile(n, t):
                tau = n * T + t
                wait(act, dve_m, tau + 1)
                wait(act, dve_p, tau - 1)
                act.activation(ex[:, t % 2], p_s[:, t % 2], ACT.Exp, bias=neg_max[:, t % 2],
                               accum_out=rowsum[:, t % 2]).then_inc(act_e, 1)

            def pair(i, more_x=True):
                for s in range(2):
                    n = 2 * i + s
                    project = not (is_last(i) and s == 1)
                    for t in range(T):
                        if 1 <= t <= 6 and project:
                            hi_g(n + 1, 1 - s, t - 1)
                        if t == 1 and not (is_first(i) and s == 0):
                            hi_cs(n - 1)
                        if s == 0 and not is_first(i):
                            if t == 1:
                                hi_wo(n - 2, 0, i)
                            if t == 2:
                                hi_val(n - 2, 0, i)
                            if t == 4:
                                hi_wo(n - 1, 1, i)
                            if t == 5:
                                hi_val(n - 1, 1, i)
                        if t in (3, 5, 7) and not is_last(i):
                            hi_w(n + 2, (t - 3) // 2)
                        if t == 6 and s == 0 and more_x:
                            hi_x(T + i, H * (i >> 3) + 1)
                        exp_tile(n, t)

            for k in range(T):
                wait(act, in_first[k], 16)
                act.copy(xt[:, 0, HI, :, k * P:k * P + P], first_x[k]).then_inc(act_x, 1)
                if k in W_AFTER:
                    hi_w(0, W_AFTER.index(k))
            for g in range(2):
                hi_g(0, 0, g)
            hi_w(1, Q)
            for g in range(2, 4):
                hi_g(0, 0, g)
            hi_w(1, K)
            for g in range(4, 6):
                hi_g(0, 0, g)
            hi_w(1, V)
            pairs(act, pair)
            hi_cs(M - 1)
            hi_wo(M - 2, 0, PAIRS)
            hi_wo(M - 1, 1, PAIRS)
            hi_val(M - 2, 0, PAIRS)
            hi_val(M - 1, 1, PAIRS)

        @block.vector
        def _(dve):
            def max_tile(n, t):
                wait(dve, pe_s, n * T + t + 1)
                dve.tensor_reduce(neg_max[:, t % 2], p_s[:, t % 2], AX_X, ALU.max, negate=True)\
                    .then_inc(dve_m, 1)

            def add_tile(n, t):
                tau = n * T + t
                wait(dve, act_e, tau + 1)
                dve.reciprocal(inv[:, t % 2], rowsum[:, t % 2]).then_inc(dve_r, 1)
                wait(dve, dve_r, tau + 1)
                if t == 0:
                    wait(dve, act_cs, n)
                    wait(dve, dve_cs, n)
                    dve.tensor_scalar(colsum[:], ex[:, 0], inv[:, 0], None, ALU.mult).then_inc(dve_p, 1)
                else:
                    wait(dve, dve_p, tau)
                    dve.scalar_tensor_tensor(out=colsum[:], in0=ex[:, t % 2], scalar=inv[:, t % 2],
                                             in1=colsum[:], op0=ALU.mult, op1=ALU.add).then_inc(dve_p, 1)

            def lo_g(m, par, g):
                r, half = divmod(g, 2)
                at = slice(half * NB, half * NB + NB)
                wait(dve, act_g, G * m + g + 1)
                dve.scalar_tensor_tensor(out=qk[:, par, r, LO, at], in0=p_g[:, g % 2],
                                         scalar=SCALE if r == Q else 1.0,
                                         in1=rounded(qk[:, par, r, HI, at]),
                                         op0=ALU.mult, op1=ALU.subtract).then_inc(dve_g, 1)

            def lo_cs(m):
                wait(dve, act_cs, m + 1)
                dve.tensor_tensor(cs[:, LO], colsum[:], rounded(cs[:, HI]), ALU.subtract).then_inc(dve_cs, 1)

            def times_v(m, par):
                wait(dve, act_g, G * (m + 1))
                wait(dve, act_val, m - 1)
                wait(dve, dve_val, m - 1)
                for half in range(2):
                    at = slice(half * NB, half * NB + NB)
                    wait(dve, pe_cs, 2 * m + half + 1)
                    dve.tensor_tensor(val[:, par, at], v_sb[:, par, at], p_o[:, half], ALU.mult)\
                        .then_inc(dve_v, 1)

            def lo_val(m, r):
                wait(dve, act_val, m + 1)
                dve.tensor_tensor(val2[:, r, LO], val[:, r], rounded(val2[:, r, HI]), ALU.subtract)\
                    .then_inc(dve_val, 1)

            def add_y(i, j):
                wait(dve, pe_o, T * (i - 1) + j + 1)
                wait(dve, in_y[j], 16 * (((i - 1) >> 3) + 1))
                dve.tensor_tensor(y_sb[:, j], y_sb[:, j], p_o[:, j % 2], ALU.add).then_inc(dve_y, 1)

            def pair(i, more_x=True):
                for s in range(2):
                    n = 2 * i + s
                    project = not (is_last(i) and s == 1)
                    for t in range(T):
                        if t == 7 and not is_first(i):
                            add_y(i, 4 * s)
                            add_y(i, 4 * s + 1)
                        if t == 0:
                            if s == 0 and not (isinstance(i, int) and i <= 1):
                                add_y(i - 1, 6)
                                add_y(i - 1, 7)
                            if s == 1 and not is_first(i):
                                add_y(i, 2)
                                add_y(i, 3)
                        max_tile(n, t)
                        if t == 0 and not (is_first(i) and s == 0):
                            add_tile(n - 1, T - 1)
                        if 1 <= t <= 4 and project:
                            lo_g(n + 1, 1 - s, t - 1)
                        if t == 1 and not (is_first(i) and s == 0):
                            lo_cs(n - 1)
                        if t == 3 and not (is_first(i) and s == 0):
                            times_v(n - 1, 1 - s)
                        if s == 0 and not is_first(i):
                            if t == 2:
                                lo_val(n - 2, 0)
                            if t == 5:
                                lo_val(n - 1, 1)
                        if t >= 1:
                            add_tile(n, t - 1)

            dve.memset(ones_f[:], 1.0).then_inc(dve_1, 1)
            dve.wait_ge(dve_1, 1)
            dve.tensor_copy(ones[:], ones_f[:]).then_inc(dve_1, 1)
            for k in range(T):
                at = slice(k * P, k * P + P)
                wait(dve, act_x, k + 1)
                dve.tensor_tensor(xt[:, 0, LO, :, at], first_x[k], rounded(xt[:, 0, HI, :, at]),
                                  ALU.subtract).then_inc(pool_x, 1)
            for g in range(4):
                lo_g(0, 0, g)
            pairs(dve, pair)
            add_tile(M - 1, T - 1)
            add_y(PAIRS - 1, 6)
            add_y(PAIRS - 1, 7)
            lo_cs(M - 1)
            times_v(M - 1, 1)
            lo_val(M - 2, 0)
            lo_val(M - 1, 1)
            norm1.turn(dve, 0)
            norm1.read(dve, 0, 0)
            for j in range(T):
                if j == 1:
                    norm1.scale(dve)
                if j in (3, 5):
                    norm1.write(dve, 0, range(j - 3, j - 1))
                add_y(PAIRS, j)

        @block.tensor
        def _(pe):
            def project(m, par, g, batch_par):
                r, half = divmod(g, 2)
                wait(pe, pool_w, 3 * m + r + 1)
                wait(pe, act_g, G * m + g - 1)
                if g >= 2:
                    wait(pe, dve_g, 4 * m + g - 1)
                for c in range(C):
                    for a, b in PASSES:
                        ins = pe.matmul(p_g[:, g % 2], w_sb[:, a, r, c],
                                        xt_part(batch_par, b, c, half * NB, NB),
                                        start=(c == 0 and (a, b) == PASSES[0]),
                                        stop=(c == C - 1 and (a, b) == PASSES[-1]))
                ins.then_inc(pe_g, 1)

            def scores(n, par, t):
                if t == 0:
                    wait(pe, dve_g, 4 * (n + 1))
                wait(pe, act_e, n * T + t - 1)
                at = slice(t * P, t * P + P)
                for a, b in PASSES:
                    for half in range(HALVES):
                        keys = slice(half * NB, half * NB + NB)
                        ins = pe.matmul(p_s[:, t % 2, keys], qk[:, par, Q, a, at], qk[:, par, K, b, keys],
                                        start=((a, b) == PASSES[0]), stop=((a, b) == PASSES[-1]))
                ins.then_inc(pe_s, 1)

            def spread(m):
                wait(pe, dve_cs, m + 1)
                for half in range(HALVES):
                    at = slice(half * NB, half * NB + NB)
                    for part in (HI, LO):
                        ins = pe.matmul(p_o[:, half], ones[:], cs[:, part, at],
                                        start=(part == HI), stop=(part == LO))
                    ins.then_inc(pe_cs, 1)

            def out_tile(i, j):
                wait(pe, dve_val, 2 * i)
                wait(pe, pool_wo, 2 * i)
                if j % 4 >= 2:
                    wait(pe, dve_y, T * (i - 1) + j - 1)
                at = slice(j * P, j * P + P)
                for r in range(2):
                    for a, b in PASSES:
                        ins = pe.matmul(p_o[:, j % 2], val2[:, r, a, at], wo_sb[:, r, b],
                                        start=(r == 0 and (a, b) == PASSES[0]),
                                        stop=(r == 1 and (a, b) == PASSES[-1]))
                ins.then_inc(pe_o, 1)

            def pair(i, more_x=True):
                for s in range(2):
                    n = 2 * i + s
                    batch_par = ((i + s) >> 3) & 1
                    for t in range(T):
                        scores(n, s, t)
                        if t == 0 and not (is_last(i) and s == 1):
                            wait(pe, pool_x, T * (((i + s) >> 3) + 1))
                        if t < G and not (is_last(i) and s == 1):
                            project(n + 1, 1 - s, t, batch_par)
                        if t == 2 and not (is_first(i) and s == 0):
                            if not is_first(i):
                                wait(pe, dve_y, T * (i - 1) if s == 0 else T * (i - 1) + 4)
                            spread(n - 1)
                        if t >= 6 and not is_first(i):
                            if t == 6:
                                wait(pe, dve_v, 2 * n)
                            out_tile(i, 4 * s + 2 * (t - 6))
                            out_tile(i, 4 * s + 2 * (t - 6) + 1)

            for g in range(G):
                if g < 2:
                    wait(pe, pool_x, T // 2 * (g + 1))
                project(0, 0, g, 0)
            pe.wait_ge(dve_1, 2)
            pair(0)
            pair(1)
            with pe.Fori(2, PAIRS - 1) as i:
                pair(i)
            pair(PAIRS - 1)
            pe.wait_ge(dve_y, T * (PAIRS - 1))
            spread(M - 1)
            pe.wait_ge(dve_v, 2 * M)
            for j in range(T):
                if j in (4, 5):
                    pe.wait_ge(dve_y, T * (PAIRS - 1) + j - 1)
                out_tile(PAIRS, j)


class Chain:

    def __init__(self, eng, sem, per):
        self.eng, self.sem, self.per, self.base, self.n = eng, sem, per, 0, 0

    def turn(self, k):
        self.base, self.n = k * self.per, 0

    def then(self, ins):
        ins.then_inc(self.sem, 1)
        self.n += 1

    def settle(self):
        self.eng.wait_ge(self.sem, self.base + self.n)

    def settle_idle(self, spare):
        self.settle()
        self.eng.memset(spare, 0.0)

    def step(self, ins):
        self.then(ins)
        self.settle()

    def close(self):
        assert self.n == self.per, (self.n, self.per)


RSQRT_SEED = 0x5F3759DF
NEWTON = 3


def ln_rsqrt(dve, link, eps, var, v, g, a):
    link.step(dve.tensor_scalar(v, var, eps, None, ALU.add))
    link.step(dve.tensor_scalar(a.bitcast(U32), v.bitcast(U32), 1, None, ALU.logical_shift_right))
    link.step(dve.tensor_scalar(g.bitcast(U32), a.bitcast(U32), -1.0, float(RSQRT_SEED), ALU.mult, ALU.add))
    for _ in range(NEWTON):
        link.step(dve.scalar_tensor_tensor(out=a, in0=g, scalar=-0.5, in1=g, op0=ALU.mult, op1=ALU.mult))
        link.step(dve.tensor_tensor(a, a, v, ALU.mult))
        link.step(dve.scalar_tensor_tensor(out=g, in0=a, scalar=1.5, in1=g, op0=ALU.add, op1=ALU.mult))


class Norm1:
    EPS = 1e-5

    def __init__(self, nc, ctx, D):
        def sb(name, shape, dt=F32):
            return ctx.enter_context(nc.sbuf_tensor(name, shape, dt))

        def sem(name):
            return ctx.enter_context(nc.semaphore(name))

        self.TT = TT = NB // P
        self.y = [sb("y_even", [P, TT, D])]
        self.x2 = [sb("x2_even", [P, TT, D])]
        self.bn = sb("bn", [P, TT, 6])
        self.mv = sb("mv", [P, TT, 2])
        self.small = sb("small", [P, 3, TT])
        self.spare = sb("spare", [P, 1])
        self.in_y = [sem(f"in_yb{q}") for q in range(2)]
        self.ln_c = sem("ln_c")
        self.dve_ln = sem("dve_ln")

    def load(self, sp, y, c, par):
        y_v = y.rearrange("(c j p) d -> p c j d", p=P, j=self.TT)
        sp.dma_start(self.y[par][:], y_v[:, bass.ds(c, 1)].rearrange("p o j d -> p (o j) d"))\
            .then_inc(self.in_y[par], 16)

    def turn(self, dve, c):
        self.link = Chain(dve, self.ln_c, 2 * self.TT + 3 + 3 * NEWTON)
        self.link.turn(c)

    def read(self, dve, c, par):
        wait(dve, self.in_y[par], 16 * ((c >> 1) + 1))
        for j in range(self.TT):
            self.link.then(dve.bn_stats(self.bn[:, j], self.y[par][:, j]))
        self.link.settle_idle(self.spare[:])
        for j in range(self.TT):
            self.link.then(dve.bn_aggr(self.mv[:, j], self.bn[:, j]))
        self.link.settle()

    def scale(self, dve):
        ln_rsqrt(dve, self.link, self.EPS, self.mv[:, :, 1], self.small[:, 0], self.small[:, 1], self.small[:, 2])
        self.link.close()

    def write(self, dve, par, tiles):
        for j in tiles:
            dve.tensor_scalar(self.x2[par][:, j], self.y[par][:, j], self.mv[:, j, 0:1], self.small[:, 1, j:j + 1],
                              ALU.subtract, ALU.mult).then_inc(self.dve_ln, 1)


class Handover:

    def __init__(self, nc, ctx, E, D, I, C_SLOTS):
        self.HALF = C_SLOTS // 2
        self.KC, self.IC = D // P, I // P
        self.GU = 2 * self.KC * I
        self.WORDS = self.GU + self.IC * D

        def sb(name, shape, dt=F32):
            return ctx.enter_context(nc.sbuf_tensor(name, shape, dt))

        def sem(name):
            return ctx.enter_context(nc.semaphore(name))

        self.ident = sb("ident", [P, P])
        self.raw = sb("raw", [P, 2, self.WORDS])
        self.slots = sb("slots", [self.HALF, 2 * E, 2])
        self.ab = sb("ab", [P, NB // P, D])
        self.xg = sb("xg", [self.HALF, 2, 2, D])
        self.in_w = [[sem(f"in_ew{q}{r}") for r in range(3)] for q in range(2)]
        self.in_t = sem("in_t")
        self.out_a = sem("out_a")
        self.pool_x = sem("pool_x0")

    def gate_up(self, par):
        return self.raw[:, par, 0:self.GU].rearrange("p (r k i) -> p r k i", r=2, k=self.KC)

    def down(self, par):
        return self.raw[:, par, self.GU:].rearrange("p (k d) -> p k d", k=self.IC)

    def load(self, sp, weights, e, par, r):
        to = self.down(par) if r == 2 else self.gate_up(par)[:, r]
        sp.dma_start(to, weights[r].rearrange("e (k p) i -> p e k i", p=P)[:, bass.ds(e, 1)]
                     .rearrange("p o k i -> p (o k) i")).then_inc(self.in_w[par][r], 16)


def route_and_share(nc, norm1, ready, y, router_wT, e_bias, gate_T, up_T, down_T, weights, x2, acc, table, C_SLOTS):
    ident = ready.ident
    N, D = y.shape
    E = router_wT.shape[1]
    I = gate_T.shape[1]
    KC, IC = D // P, I // P
    TT = NB // P
    TURNS = N // NB
    TOPK, NG, TKG, GE, ROUTED = 4, 8, 3, E // 8, 2.5
    HALF = C_SLOTS // 2
    COLS = 2 * E
    NOBODY = 2.0 * N
    assert KC == 4 and IC == 4 and GE == 4

    with ExitStack() as ctx:
        def sb(name, shape, dt=F32):
            return ctx.enter_context(nc.sbuf_tensor(name, shape, dt))

        def ps(name, shape):
            return ctx.enter_context(nc.psum_tensor(name, shape, F32))

        def sem(name):
            return ctx.enter_context(nc.semaphore(name))

        def rounded(tile):
            return tile.bitcast(F32)

        r_raw = sb("r_raw", [P, KC, E])
        r_sb = sb("r_sb", [P, KC, 2, E], F32R)
        assert 2 * ready.WORDS == 3 * KC * I
        s_raw = ready.raw[:].rearrange("p a w -> p (a w)").rearrange("p (r k i) -> p r k i", r=3, k=KC)
        s_sb = sb("s_sb", [P, 2, 3, KC, I], F32R)
        xb = norm1.x2
        norm1.y.append(sb("y_odd", [P, TT, D]))
        xb.append(sb("x2_odd", [P, TT, D]))
        xT2 = sb("xT2", [P, 2, 2, KC, NB], F32R)
        sg = sb("sg", [P, 2, NB])
        hf = sb("hf", [P, 2, NB])
        hb = sb("hb", [P, 2, IC, NB], F32R)
        ab = ready.ab
        before = sb("before", [P, P], BF16)
        every = sb("every", [P, P], BF16)
        iota_e = sb("iota_e", [P, E])
        iota_g = sb("iota_g", [P, NG])
        bias = sb("bias", [P, E])
        empty = sb("empty", [P, COLS * HALF // P, 2])
        spare = norm1.spare
        idle = sb("idle", [P, 1])
        logit = sb("logit", [P, TT, E])
        prob = sb("prob", [P, TT, E])
        sc = sb("sc", [P, TT, E])
        pair_hi = sb("pair_hi", [P, TT * NG, 2])
        pair_lo = sb("pair_lo", [P, TT * NG, 2])
        top1 = sb("top1", [P, TT * NG])
        top2 = sb("top2", [P, TT * NG])
        top2b = sb("top2b", [P, TT * NG])
        gscore = sb("gscore", [P, TT, NG])
        g8 = sb("g8", [P, TT, 8])
        gi = sb("gi", [P, TT, 8], U32)
        g_hot = sb("g_hot", [P, TT, TKG, NG])
        g_mask = sb("g_mask", [P, TT, NG])
        masked = sb("masked", [P, TT, E])
        e8 = sb("e8", [P, TT, 8])
        ei = sb("ei", [P, TT, 8], U32)
        hot = sb("hot", [P, TT, TOPK, E])
        chosen = sb("chosen", [P, TT, E], BF16)
        tmp = sb("tmp", [P, TT, TOPK, E])
        wk = sb("wk", [P, TT, TOPK])
        wsum = sb("wsum", [P, TT])
        winv = sb("winv", [P, TT])
        taken = sb("taken", [P, E])
        pos = sb("pos", [P, TT, E])
        pos_k = sb("pos_k", [P, TT, TOPK])
        second = sb("second", [P, TT, TOPK])
        column = sb("column", [P, TT, TOPK])
        slot = sb("slot", [P, 2, TT, TOPK], U32)
        token = sb("token", [P, TT, TOPK])
        entry = sb("entry", [P, 2, TT, TOPK, 2])

        p_t = ps("p_t", [P, 2, KC, P])
        p_r = ps("p_r", [P, TT, 2, E])
        p_c = ps("p_c", [P, NB])
        p_f = ps("p_f", [P, 2, 2, NB])

        in_r = sem("in_r")
        in_s = [sem(f"in_s{r}") for r in range(3)]
        in_b = sem("in_b")
        out_e = sem("out_e")
        out_x = [sem(f"out_x{r}") for r in range(2)]
        out_a = ready.out_a
        out_t = [sem(f"out_t{r}") for r in range(2)]
        act_s = sem("act_s")
        dve_s = sem("dve_s")
        pool_c = sem("pool_c")
        pool_i = sem("pool_i")
        ro_c = sem("ro_c")
        dve_ln = norm1.dve_ln
        pe_t = sem("pe_t")
        act_t = sem("act_t")
        dve_t = sem("dve_t")
        pe_r = sem("pe_r")
        dve_r = sem("dve_r")
        act_r = sem("act_r")
        dve_m = sem("dve_mm")
        pe_c = sem("pe_c")
        dve_e = sem("dve_e")
        pe_f = sem("pe_f")
        act_f = sem("act_f")
        dve_f1 = sem("dve_f1")
        dve_f = sem("dve_f")
        act_h = sem("act_h")
        dve_h = sem("dve_h")
        pe_d = sem("pe_d")
        dve_a = sem("dve_a")

        x2_v = x2.rearrange("(c j p) d -> p c j d", p=P, j=TT)
        acc_v = acc.rearrange("(c j p) d -> p c j d", p=P, j=TT)

        def turns(body, eng):
            body(0, 0)
            body(1, 1)
            with eng.Fori(1, TURNS // 2 - 1) as cc:
                body(2 * cc, 0)
                body(2 * cc + 1, 1)
            body(TURNS - 2, 0)
            body(TURNS - 1, 1)

        def is_last(c):
            return isinstance(c, int) and c == TURNS - 1

        block = ctx.enter_context(nc.Block())

        @block.sync
        def _(sp):
            def load_y(c, par):
                wait(sp, dve_ln, TT * (c - 1))
                norm1.load(sp, y, c, par)

            def store_x(c, par):
                wait(sp, dve_ln, TT * (c + 1))
                sp.dma_start(x2_v[:, bass.ds(c, 1)].rearrange("p o j d -> p (o j) d"), xb[par][:])\
                    .then_inc(out_x[par], 16)

            sp.dma_start(r_raw[:], router_wT.rearrange("(k p) e -> p k e", p=P)).then_inc(in_r, 16)
            for r, w in enumerate((gate_T, up_T, down_T)):
                if r == 2:
                    load_y(1, 1)
                sp.dma_start(s_raw[:, r], w.rearrange("(k p) i -> p k i", p=P)).then_inc(in_s[r], 16)
            sp.dma_start(bias[:], e_bias.partition_broadcast(P)).then_inc(in_b, 16)
            sp.wait_ge(pool_c, 3)
            sp.dma_start(table.rearrange("(p n) w -> p n w", p=P), empty[:]).then_inc(out_e, 16)
            store_x(0, 0)
            sp.wait_ge(dve_s, 4)
            for e in range(2):
                for r in range(3):
                    ready.load(sp, weights, e, e, r)

            def body(c, par):
                if not (isinstance(c, int) and c + 2 >= TURNS):
                    load_y(c + 2, par)
                if not is_last(c):
                    store_x(c + 1, 1 - par)
                if is_last(c):
                    for q in range(2):
                        sp.wait_ge(out_x[q], 16 * (TURNS // 2))
                        sp.wait_ge(out_t[q], 16 * TT * TOPK * (TURNS // 2))
                    sp.dma_start(ready.slots[:], table.rearrange("(p n) w -> p n w", p=HALF))\
                        .then_inc(ready.in_t, 16)
                wait(sp, dve_a, TT * (c + 1))
                sp.dma_start(acc_v[:, bass.ds(c, 1)].rearrange("p o j d -> p (o j) d"), ab[:])\
                    .then_inc(out_a, 16)

            turns(body, sp)

        @block.gpsimd
        def _(pool):
            pool.memset(ident[:], 0.0).then_inc(pool_c, 1)
            pool.memset(every[:], 1.0).then_inc(pool_c, 1)
            pool.memset(empty[:], NOBODY).then_inc(pool_c, 1)
            pool.wait_ge(pool_c, 2)
            pool.affine_select(out=ident[:], in_=ident[:], compare_op=ALU.not_equal, fill=1.0, base=0,
                               pattern=[[-1, P]], channel_multiplier=1).then_inc(pool_c, 1)
            pool.affine_select(out=before[:], in_=every[:], compare_op=ALU.is_gt, fill=0.0, base=0,
                               pattern=[[1, P]], channel_multiplier=-1).then_inc(pool_c, 1)
            pool.iota(iota_e[:], [[1, E]], base=0, channel_multiplier=0,
                      allow_small_or_imprecise_dtypes=True).then_inc(pool_c, 1)
            pool.iota(iota_g[:], [[1, NG]], base=0, channel_multiplier=0,
                      allow_small_or_imprecise_dtypes=True).then_inc(pool_c, 1)
            pool.iota(token[:], [[P, TT], [0, TOPK]], base=-NB, channel_multiplier=1,
                      allow_small_or_imprecise_dtypes=True).then_inc(pool_c, 1)
            pool.memset(taken[:], 0.0).then_inc(pool_c, 1)
            pool.memset(ready.xg[:], 0.0).then_inc(ready.pool_x, 1)
            pool.wait_ge(pool_c, 4)
            pool.wait_ge(out_e, 16)

            def body(c, par):
                wait(pool, dve_e, c + 1)
                wait(pool, pool_i, c)
                pool.tensor_tensor(idle[:], ident[:, 0:1], ident[:, 0:1], ALU.mult).then_inc(pool_i, 1)
                for j in range(TT):
                    for k in range(TOPK):
                        pool.indirect_dma_start(
                            table, bass.IndirectOffsetOnAxis(slot[:, par, j, k:k + 1], 0), entry[:, par, j, k], None,
                            bounds_check=C_SLOTS * E - 1, oob_is_err=False).then_inc(out_t[par], 16)

            turns(body, pool)

        @block.scalar
        def _(act):
            act.wait_ge(in_r, 16)
            act.copy(r_sb[:, :, HI], r_raw[:]).then_inc(act_s, 1)

            def hi_t(c, par, j):
                wait(act, pe_t, TT * c + j + 1)
                if j == 0:
                    wait(act, pe_f, IC * (c - 1))
                act.copy(xT2[:, par, HI, :, j * P:j * P + P], p_t[:, j % 2]).then_inc(act_t, 1)

            def sigmoid_r(c):
                wait(act, dve_r, c + 1)
                wait(act, dve_m, c)
                act.activation(prob[:], logit[:], ACT.Sigmoid).then_inc(act_r, 1)

            for j in range(TT):
                hi_t(0, 0, j)
            for r in range(3):
                act.wait_ge(in_s[r], 16)
                act.copy(s_sb[:, HI, r], s_raw[:, r]).then_inc(act_s, 1)
                if r == 1:
                    sigmoid_r(0)

            def body(c, par):
                for f in range(IC):
                    wait(act, pe_f, IC * c + f + 1)
                    if f < 2:
                        wait(act, dve_f1, IC * c + f - 1)
                    act.activation(sg[:, f % 2], p_f[:, f % 2, 0], ACT.Sigmoid).then_inc(act_f, 1)
                    wait(act, dve_f, IC * c + f + 1)
                    if f == 0:
                        wait(act, pe_d, TT * c)
                    act.copy(hb[:, HI, f], hf[:, f % 2]).then_inc(act_h, 1)
                    if f in (1, 2) and not is_last(c):
                        hi_t(c + 1, 1 - par, 2 * f - 2)
                        hi_t(c + 1, 1 - par, 2 * f - 1)
                if not is_last(c):
                    sigmoid_r(c + 1)

            turns(body, act)

        @block.vector
        def _(dve):
            ro = Chain(dve, ro_c, 46)

            def norm(c, par):
                wait(dve, out_x[par], 16 * (c >> 1))
                wait(dve, pe_t, TT * (c - 1))
                norm1.turn(dve, c)
                norm1.read(dve, c, par)
                norm1.scale(dve)
                norm1.write(dve, par, range(TT))

            def lo_t(c, par, j):
                wait(dve, act_t, TT * c + j + 1)
                at = slice(j * P, j * P + P)
                dve.tensor_tensor(xT2[:, par, LO, :, at], p_t[:, j % 2], rounded(xT2[:, par, HI, :, at]),
                                  ALU.subtract).then_inc(dve_t, 1)

            def add_logits(c):
                wait(dve, pe_r, c + 1)
                wait(dve, act_r, c)
                dve.tensor_reduce(logit[:], p_r[:].rearrange("p t a e -> p t e a"), AX_X, ALU.add).then_inc(dve_r, 1)

            def choose_groups(c, par):
                ro.turn(c)
                tt = dve.tensor_tensor
                wait(dve, act_r, c + 1)
                wait(dve, pe_c, c)
                wait(dve, out_t[par], 16 * TT * TOPK * (c >> 1))
                ro.step(tt(sc[:], prob[:], bias[:].unsqueeze(1).to_broadcast([P, TT, E]), ALU.add))
                quad = sc[:].rearrange("p t (g q i) -> p (t g) q i", q=2, i=2)
                ro.then(tt(pair_hi[:], quad[:, :, :, 0], quad[:, :, :, 1], ALU.max))
                ro.step(tt(pair_lo[:], quad[:, :, :, 0], quad[:, :, :, 1], ALU.min))
                ro.then(tt(top1[:], pair_hi[:, :, 0], pair_hi[:, :, 1], ALU.max))
                ro.then(tt(top2[:], pair_hi[:, :, 0], pair_hi[:, :, 1], ALU.min))
                ro.step(tt(top2b[:], pair_lo[:, :, 0], pair_lo[:, :, 1], ALU.max))
                ro.step(tt(top2[:], top2[:], top2b[:], ALU.max))
                ro.then(tt(gscore[:].rearrange("p t g -> p (t g)"), top1[:], top2[:], ALU.add))
                ro.settle_idle(spare[:])
                for j in range(TT):
                    ro.then(dve.max(g8[:, j], gscore[:, j]))
                ro.settle_idle(spare[:])
                for j in range(TT):
                    ro.then(dve.max_index(gi[:, j], g8[:, j], gscore[:, j]))
                ro.settle()

            def choose_experts(c, par):
                tt = dve.tensor_tensor
                ro.step(tt(g_hot[:], gi[:, :, 0:TKG].unsqueeze(3).to_broadcast([P, TT, TKG, NG]),
                           iota_g[:].unsqueeze(1).unsqueeze(1).to_broadcast([P, TT, TKG, NG]), ALU.is_equal))
                ro.step(dve.tensor_reduce(g_mask[:], g_hot[:].rearrange("p t k g -> p t g k"), AX_X, ALU.max))
                ro.then(tt(masked[:].rearrange("p t (g i) -> p (t g) i", i=GE),
                           sc[:].rearrange("p t (g i) -> p (t g) i", i=GE),
                           g_mask[:].rearrange("p t g -> p (t g)").unsqueeze(2).to_broadcast([P, TT * NG, GE]),
                           ALU.mult))
                ro.settle_idle(spare[:])
                for j in range(TT):
                    ro.then(dve.max(e8[:, j], masked[:, j]))
                ro.settle_idle(spare[:])
                for j in range(TT):
                    ro.then(dve.max_index(ei[:, j], e8[:, j], masked[:, j]))
                ro.settle()

            def weigh(c, par):
                tt, ts = dve.tensor_tensor, dve.tensor_scalar
                ro.step(tt(hot[:], ei[:, :, 0:TOPK].unsqueeze(3).to_broadcast([P, TT, TOPK, E]),
                           iota_e[:].unsqueeze(1).unsqueeze(1).to_broadcast([P, TT, TOPK, E]), ALU.is_equal))
                ro.then(dve.tensor_reduce(chosen[:], hot[:].rearrange("p t k e -> p t e k"), AX_X, ALU.max))
                ro.step(tt(tmp[:], hot[:], prob[:].unsqueeze(2).to_broadcast([P, TT, TOPK, E]), ALU.mult))
                ro.step(dve.tensor_reduce(wk[:], tmp[:], AX_X, ALU.add))
                dve.nop().then_inc(dve_m, 1)
                ro.step(dve.tensor_reduce(wsum[:], wk[:], AX_X, ALU.add))
                ro.step(ts(winv[:], wsum[:], 1e-20, None, ALU.add))
                ro.step(dve.reciprocal(wsum[:], winv[:]))
                ro.step(tt(wk[:], wk[:], wsum[:].unsqueeze(2).to_broadcast([P, TT, TOPK]), ALU.mult))
                ro.then(ts(entry[:, par, :, :, 1], wk[:], ROUTED, None, ALU.mult))
                ro.step(ts(token[:], token[:], float(NB), None, ALU.add))
                ro.then(dve.tensor_copy(entry[:, par, :, :, 0], token[:]))

            def place(c, par):
                tt, ts, stt = dve.tensor_tensor, dve.tensor_scalar, dve.scalar_tensor_tensor
                counts = p_c[:, 0:(TT + 1) * E].rearrange("p (t e) -> p t e", e=E)
                wait(dve, pe_c, c + 1)
                ro.step(tt(pos[:], counts[:, 0:TT], taken[:].unsqueeze(1).to_broadcast([P, TT, E]), ALU.add))
                ro.then(tt(taken[:], taken[:], counts[:, TT], ALU.add))
                ro.step(tt(tmp[:], hot[:], pos[:].unsqueeze(2).to_broadcast([P, TT, TOPK, E]), ALU.mult))
                ro.step(dve.tensor_reduce(pos_k[:], tmp[:], AX_X, ALU.add))
                ro.then(ts(second[:], pos_k[:], float(HALF), None, ALU.is_ge))
                ro.step(ts(column[:], ei[:, :, 0:TOPK], 2.0, None, ALU.mult))
                ro.step(stt(out=column[:], in0=second[:], scalar=float(1 - HALF * COLS), in1=column[:],
                            op0=ALU.mult, op1=ALU.add))
                ro.step(stt(out=slot[:, par], in0=pos_k[:], scalar=float(COLS), in1=column[:],
                            op0=ALU.mult, op1=ALU.add))
                dve.nop().then_inc(dve_e, 1)
                ro.close()

            def hidden(c, f):
                wait(dve, act_f, IC * c + f + 1)
                dve.tensor_tensor(hf[:, f % 2], sg[:, f % 2], p_f[:, f % 2, 0], ALU.mult).then_inc(dve_f1, 1)
                wait(dve, dve_f1, IC * c + f + 1)
                dve.tensor_tensor(hf[:, f % 2], hf[:, f % 2], p_f[:, f % 2, 1], ALU.mult).then_inc(dve_f, 1)
                wait(dve, act_h, IC * c + f + 1)
                dve.tensor_tensor(hb[:, LO, f], hf[:, f % 2], rounded(hb[:, HI, f]), ALU.subtract)\
                    .then_inc(dve_h, 1)

            dve.wait_ge(act_s, 1)
            dve.tensor_tensor(r_sb[:, :, LO], r_raw[:], rounded(r_sb[:, :, HI]), ALU.subtract).then_inc(dve_s, 1)
            for j in range(TT):
                lo_t(0, 0, j)
            for r in range(3):
                if r == 2:
                    add_logits(0)
                dve.wait_ge(act_s, 2 + r)
                dve.tensor_tensor(s_sb[:, LO, r], s_raw[:, r], rounded(s_sb[:, HI, r]), ALU.subtract)\
                    .then_inc(dve_s, 1)
            dve.wait_ge(pool_c, 9)
            dve.wait_ge(in_b, 16)

            def body(c, par):
                if is_last(c):
                    choose_groups(c, par)
                    choose_experts(c, par)
                    weigh(c, par)
                    hidden(c, 0)
                    place(c, par)
                    hidden(c, 1)
                    hidden(c, 2)
                    hidden(c, 3)
                else:
                    norm(c + 1, 1 - par)
                    hidden(c, 0)
                    choose_groups(c, par)
                    hidden(c, 1)
                    lo_t(c + 1, 1 - par, 0)
                    lo_t(c + 1, 1 - par, 1)
                    choose_experts(c, par)
                    hidden(c, 2)
                    lo_t(c + 1, 1 - par, 2)
                    lo_t(c + 1, 1 - par, 3)
                    weigh(c, par)
                    hidden(c, 3)
                    add_logits(c + 1)
                wait(dve, out_a, 16 * c)
                for j in range(TT):
                    wait(dve, pe_d, TT * c + j + 1)
                    dve.tensor_tensor(ab[:, j], xb[par][:, j], p_f[:, j // 2, j % 2], ALU.add)\
                        .then_inc(dve_a, 1)
                    if j == 1 and not is_last(c):
                        place(c, par)

            turns(body, dve)

        @block.tensor
        def _(pe):
            def turn(c, par, j):
                wait(pe, dve_ln, TT * c + j + 1)
                wait(pe, dve_t, TT * c + j - 1)
                for k in range(KC):
                    ins = pe.transpose(p_t[:, j % 2, k], xb[par][:, j, k * P:k * P + P], ident[:])
                ins.then_inc(pe_t, 1)

            def logits(c, par):
                wait(pe, dve_t, TT * (c + 1))
                wait(pe, dve_r, c)
                for j in range(TT):
                    at = slice(j * P, j * P + P)
                    for k in range(KC):
                        pe.matmul(p_r[:, j], xT2[:, par, HI, k, at], r_sb[:, k], start=(k == 0), stop=False)
                        ins = pe.matmul(p_r[:, j, 0], xT2[:, par, LO, k, at], r_sb[:, k, HI], start=False,
                                        stop=(k == KC - 1))
                ins.then_inc(pe_r, 1)

            def count(c):
                wait(pe, dve_m, c + 1)
                wait(pe, dve_e, c)
                for j in range(TT + 1):
                    out = p_c[:, j * E:j * E + E]
                    for i in range(min(j, TT)):
                        ins = pe.matmul(out, every[:], chosen[:, i], start=(i == 0),
                                        stop=(j == TT and i == TT - 1))
                    if j < TT:
                        ins = pe.matmul(out, before[:], chosen[:, j], start=(j == 0), stop=True)
                ins.then_inc(pe_c, 1)

            def gate_up(c, par, f):
                if f < 2:
                    wait(pe, dve_a, TT * (c - 1) + 2 * f + 2)
                else:
                    wait(pe, dve_f, IC * c + f - 1)
                for r in range(2):
                    for k in range(KC):
                        for a, b in PASSES:
                            ins = pe.matmul(p_f[:, f % 2, r], s_sb[:, a, r, k, f * P:f * P + P],
                                            xT2[:, par, b, k], start=(k == 0 and (a, b) == PASSES[0]),
                                            stop=(k == KC - 1 and (a, b) == PASSES[-1]))
                ins.then_inc(pe_f, 1)

            def down(j, chunks):
                for k in chunks:
                    for a, b in PASSES:
                        ins = pe.matmul(p_f[:, j // 2, j % 2], hb[:, a, k, j * P:j * P + P], s_sb[:, b, 2, k],
                                        start=(k == 0 and (a, b) == PASSES[0]),
                                        stop=(k == IC - 1 and (a, b) == PASSES[-1]))
                if k == IC - 1:
                    ins.then_inc(pe_d, 1)

            pe.wait_ge(pool_c, 9)
            for j in range(TT):
                turn(0, 0, j)
            pe.wait_ge(dve_s, 1)
            logits(0, 0)
            pe.wait_ge(dve_s, 3)

            def body(c, par):
                for f in range(IC):
                    gate_up(c, par, f)
                    if f in (1, 2) and not is_last(c):
                        turn(c + 1, 1 - par, 2 * f - 2)
                        turn(c + 1, 1 - par, 2 * f - 1)
                    if f == 1 and is_last(c):
                        count(c)
                if not is_last(c):
                    logits(c + 1, 1 - par)
                if isinstance(c, int) and c == 0:
                    pe.wait_ge(dve_s, 4)
                wait(pe, dve_h, IC * (c + 1) - 1)
                down(0, range(IC - 1))
                down(1, range(IC - 1))
                wait(pe, dve_h, IC * (c + 1))
                down(0, [IC - 1])
                down(1, [IC - 1])
                if not is_last(c):
                    count(c)
                down(2, range(IC))
                down(3, range(IC))

            turns(body, pe)


def experts(nc, ready, weights, x2, acc, C_SLOTS):
    w_gate = weights[0]
    ident, slots, xg = ready.ident, ready.slots, ready.xg
    in_w = ready.in_w
    E, D, I = w_gate.shape
    N = x2.shape[0]
    KC, IC = D // P, I // P
    HALF = C_SLOTS // 2
    assert KC == 4 and IC == 2

    with ExitStack() as ctx:
        def sb(name, shape, dt=F32):
            return ctx.enter_context(nc.sbuf_tensor(name, shape, dt))

        def ps(name, shape):
            return ctx.enter_context(nc.psum_tensor(name, shape, F32))

        def sem(name):
            return ctx.enter_context(nc.semaphore(name))

        def rounded(tile):
            return tile.bitcast(F32)

        GU = 2 * KC * I
        w_sb = sb("ew_sb", [P, 2, 2, GU + IC * D], F32R)
        who = sb("who", [HALF, 2, 2], U32)
        to = sb("to", [HALF, 2, 2], U32)
        weight = sb("weight", [HALF, 2, 2])
        xT = sb("exT", [P, 2, KC, 2, C_SLOTS], F32R)
        gu = sb("egu", [P, 2, 2, IC, C_SLOTS])
        sg = sb("esg", [P, 2, IC * C_SLOTS])
        hf = sb("ehf", [P, 2, IC * C_SLOTS])
        hb = sb("ehb", [P, 2, 2, IC * C_SLOTS], F32R)
        yo = sb("yo", [HALF, 2, 2, D])
        idle = sb("eidle", [P, 2])

        p_t = ps("ep_t", [P, 2, NB])
        p_f = ps("ep_f", [P, 2, IC, NB])
        p_y = ps("ep_y", [P, 2, NB])

        out_y = [sem(f"out_ey{h}") for h in range(2)]
        in_x = [[sem(f"in_ex{q}{h}") for h in range(2)] for q in range(2)]
        dve_i = sem("dve_i")
        pool_i = [sem(f"pool_ei{q}") for q in range(2)]
        act_wg = [sem(f"act_wg{r}") for r in range(2)]
        act_wd = sem("act_wd")
        dve_w = [sem(f"dve_ew{r}") for r in range(2)]
        dve_wd = sem("dve_ewd")
        pool_w = sem("pool_ew")
        dve_o = sem("dve_o")
        pe_t = sem("pe_et")
        act_t = sem("act_et")
        dve_t = sem("dve_et")
        pe_f = sem("pe_ef")
        dve_g = sem("dve_eg")
        act_f = sem("act_ef")
        dve_f1 = sem("dve_ef1")
        dve_f = sem("dve_ef")
        act_h = sem("act_eh")
        dve_h = sem("dve_eh")
        pe_y = sem("pe_ey")
        act_y = sem("act_ey")

        def gate_up_of(par, part=None):
            if part is None:
                return ready.gate_up(par)
            return w_sb[:, par, part, 0:GU].rearrange("p (r k i) -> p r k i", r=2, k=KC)

        def transposed(b):
            return p_t[:, b, 0:2 * C_SLOTS].rearrange("p (k s) -> p k s", k=2)

        def down_of(par, part=None):
            if part is None:
                return ready.down(par)
            return w_sb[:, par, part, GU:].rearrange("p (k d) -> p k d", k=IC)

        def split_down(eng, par, ic):
            return eng.tensor_tensor(down_of(par, LO)[:, ic], down_of(par)[:, ic],
                                     rounded(down_of(par, HI)[:, ic]), ALU.subtract)

        def by_pairs(eng, body):
            def two(e):
                body(e, 0)
                body(e + 1, 1)
            two(0)
            with eng.Fori(1, E // 2 - 2) as ee:
                two(2 * ee)
            two(E - 4)
            two(E - 2)

        def there(e):
            return not (isinstance(e, int) and e >= E)

        block = ctx.enter_context(nc.Block())


        @block.sync
        def _(sp):
            def load(e, par):
                if isinstance(e, int) and e < 2:
                    return
                for r in range(2):
                    wait(sp, act_wg[r], e - 1)
                    wait(sp, dve_w[r], e - 1)
                    ready.load(sp, weights, e, par, r)
                wait(sp, act_wd, e - 1)
                wait(sp, dve_wd, e - 1)
                wait(sp, pool_w, e - 1)
                ready.load(sp, weights, e, par, 2)

            by_pairs(sp, load)
            for h in range(2):
                sp.wait_ge(out_y[h], 16 * E)

        @block.gpsimd
        def _(pool):
            def carry(q, before):
                wait(pool, pool_i[q], before)
                pool.tensor_tensor(idle[:, q:q + 1], ident[:, 0:1], ident[:, 0:1], ALU.mult)\
                    .then_inc(pool_i[q], 1)

            def gather(e, par):
                wait(pool, dve_i, e + 1)
                wait(pool, pe_t, 2 * (e - 1))
                carry(0, e)
                for h in range(2):
                    pool.indirect_dma_start(xg[:, par, h], None, x2,
                                            bass.IndirectOffsetOnAxis(who[:, par, h:h + 1], 0),
                                            bounds_check=N - 1, oob_is_err=False).then_inc(in_x[par][h], 16)

            def lo_down(e, par):
                wait(pool, act_wd, e + 1)
                split_down(pool, par, 1).then_inc(pool_w, 1)

            def add(e, par):
                wait(pool, dve_o, e + 1)
                for h in range(2):
                    wait(pool, act_y, 2 * e + h + 1)
                    for g in range(2):
                        wait(pool, out_y[g], 16 * e)
                    carry(1, 2 * e + h)
                    pool.indirect_dma_start(acc, bass.IndirectOffsetOnAxis(to[:, par, h:h + 1], 0),
                                            yo[:, par, h], None, bounds_check=N - 1, oob_is_err=False,
                                            compute_op=ALU.add).then_inc(out_y[h], 16)

            def body(e, par):
                if there(e + 4):
                    gather(e + 4, par)
                if there(e + 1):
                    lo_down(e + 1, 1 - par)
                add(e, par)

            pool.wait_ge(ready.pool_x, 1)
            gather(0, 0)
            gather(1, 1)
            lo_down(0, 0)
            gather(2, 0)
            gather(3, 1)
            pool.wait_ge(ready.out_a, 16 * (N // NB))
            by_pairs(pool, body)

        @block.scalar
        def _(act):
            def hi_gate_up(e, par, r):
                wait(act, in_w[par][r], 16 * ((e >> 1) + 1))
                wait(act, pe_f, 2 * (e - 2) + r + 1)
                act.copy(gate_up_of(par, HI)[:, r], gate_up_of(par)[:, r]).then_inc(act_wg[r], 1)

            def hi_down(e, par):
                wait(act, in_w[par][2], 16 * ((e >> 1) + 1))
                wait(act, pe_y, 2 * (e - 1))
                act.copy(down_of(par, HI), down_of(par)).then_inc(act_wd, 1)

            def hi_x(e, par):
                for b in range(2):
                    wait(act, pe_t, 2 * e + b + 1)
                    if b == 0:
                        wait(act, pe_f, 2 * (e - 1))
                    act.copy(xT[:, par, 2 * b:2 * b + 2, HI], transposed(b)).then_inc(act_t, 1)

            def sigmoid(e, par):
                wait(act, dve_g, 2 * e + 1)
                act.activation(sg[:, par], gu[:, par, 0].rearrange("p c s -> p (c s)"), ACT.Sigmoid)\
                    .then_inc(act_f, 1)

            def hi_h(e, par):
                wait(act, dve_f, e + 1)
                wait(act, pe_y, 2 * (e - 1))
                act.copy(hb[:, par, HI], hf[:, par]).then_inc(act_h, 1)

            def weigh(e, par, h):
                wait(act, dve_o, e + 1)
                wait(act, pe_y, 2 * e + h + 1)
                wait(act, out_y[h], 16 * (e - 1))
                act.activation(yo[:, par, h], p_y[0:HALF, h], ACT.Copy, scale=weight[:, par, h:h + 1])\
                    .then_inc(act_y, 1)

            def body(e, par):
                if there(e + 2):
                    hi_x(e + 2, par)
                    hi_gate_up(e + 2, par, 1)
                if there(e + 1):
                    hi_down(e + 1, 1 - par)
                    sigmoid(e + 1, 1 - par)
                if there(e + 3):
                    hi_gate_up(e + 3, 1 - par, 0)
                weigh(e, par, 0)
                if there(e + 1):
                    hi_h(e + 1, 1 - par)
                weigh(e, par, 1)

            for e in range(2):
                for r in range(2):
                    hi_gate_up(e, e, r)
            hi_down(0, 0)
            hi_x(0, 0)
            sigmoid(0, 0)
            hi_gate_up(2, 0, 0)
            hi_h(0, 0)
            hi_x(1, 1)
            by_pairs(act, body)

        @block.vector
        def _(dve):
            def fetch(e, par):
                for h in range(2):
                    wait(dve, in_x[par][h], 16 * (e >> 1))
                dve.tensor_copy(who[:, par], slots[:, bass.ds(2 * e, 2), 0]).then_inc(dve_i, 1)

            def to_and_weight(e, par):
                for h in range(2):
                    wait(dve, out_y[h], 16 * (e - 1))
                wait(dve, act_y, 2 * (e - 1))
                dve.tensor_copy(to[:, par], slots[:, bass.ds(2 * e, 2), 0])
                dve.tensor_copy(weight[:, par], slots[:, bass.ds(2 * e, 2), 1]).then_inc(dve_o, 1)

            def lo_gate_up(e, par, r):
                wait(dve, act_wg[r], e + 1)
                dve.tensor_tensor(gate_up_of(par, LO)[:, r], gate_up_of(par)[:, r],
                                  rounded(gate_up_of(par, HI)[:, r]), ALU.subtract).then_inc(dve_w[r], 1)

            def lo_x(e, par):
                for b in range(2):
                    wait(dve, act_t, 2 * e + b + 1)
                    two = xT[:, par, 2 * b:2 * b + 2]
                    dve.tensor_tensor(two[:, :, LO], transposed(b), rounded(two[:, :, HI]),
                                      ALU.subtract).then_inc(dve_t, 1)

            def lo_down(e, par):
                wait(dve, act_wd, e + 1)
                split_down(dve, par, 0).then_inc(dve_wd, 1)

            def add_gate_up(e, par, r):
                wait(dve, pe_f, 2 * e + r + 1)
                dve.tensor_reduce(gu[:, par, r], p_f[:, r, :, 0:2 * C_SLOTS]
                                  .rearrange("p c (a s) -> p c s a", a=2), AX_X, ALU.add).then_inc(dve_g, 1)

            def times_gate(e, par):
                wait(dve, act_f, e + 1)
                dve.tensor_tensor(hf[:, par], sg[:, par], gu[:, par, 0].rearrange("p c s -> p (c s)"), ALU.mult)\
                    .then_inc(dve_f1, 1)

            def times_up(e, par):
                wait(dve, dve_f1, e + 1)
                wait(dve, dve_g, 2 * (e + 1))
                dve.tensor_tensor(hf[:, par], hf[:, par], gu[:, par, 1].rearrange("p c s -> p (c s)"), ALU.mult)\
                    .then_inc(dve_f, 1)

            def lo_h(e, par):
                wait(dve, act_h, e + 1)
                dve.tensor_tensor(hb[:, par, LO], hf[:, par], rounded(hb[:, par, HI]), ALU.subtract)\
                    .then_inc(dve_h, 1)

            def body(e, par):
                if there(e + 4):
                    fetch(e + 4, par)
                to_and_weight(e, par)
                if there(e + 2):
                    lo_x(e + 2, par)
                    lo_gate_up(e + 2, par, 1)
                if there(e + 1):
                    add_gate_up(e + 1, 1 - par, 0)
                    lo_down(e + 1, 1 - par)
                    times_gate(e + 1, 1 - par)
                    add_gate_up(e + 1, 1 - par, 1)
                    times_up(e + 1, 1 - par)
                if there(e + 3):
                    lo_gate_up(e + 3, 1 - par, 0)
                if there(e + 1):
                    lo_h(e + 1, 1 - par)

            dve.wait_ge(ready.in_t, 16)
            fetch(0, 0)
            fetch(1, 1)
            for e in range(2):
                for r in range(2):
                    lo_gate_up(e, e, r)
            lo_down(0, 0)
            lo_x(0, 0)
            fetch(2, 0)
            add_gate_up(0, 0, 0)
            times_gate(0, 0)
            add_gate_up(0, 0, 1)
            times_up(0, 0)
            lo_h(0, 0)
            lo_x(1, 1)
            fetch(3, 1)
            lo_gate_up(2, 0, 0)
            by_pairs(dve, body)

        @block.tensor
        def _(pe):
            def transposes(e, par):
                for h in range(2):
                    wait(pe, in_x[par][h], 16 * ((e >> 1) + 1))
                for b in range(2):
                    wait(pe, dve_t, 2 * (e - 1) + b + 1)
                    for k in range(2 * b, 2 * b + 2):
                        for h in range(2):
                            at = (k % 2) * C_SLOTS + h * HALF
                            ins = pe.transpose(p_t[:, b, at:at + HALF], xg[:, par, h, k * P:k * P + P],
                                               ident[0:HALF, 0:HALF])
                    ins.then_inc(pe_t, 1)

            def gate_up(e, par):
                wait(pe, dve_t, 2 * (e + 1))
                for r in range(2):
                    wait(pe, dve_w[r], e + 1)
                    wait(pe, dve_g, 2 * (e - 1) + r + 1)
                    for ic in range(IC):
                        out = p_f[:, r, ic, 0:2 * C_SLOTS]
                        for k in range(KC):
                            w = [gate_up_of(par, a)[:, r, k, ic * P:ic * P + P] for a in (HI, LO)]
                            pe.matmul(out, w[HI], xT[:, par, k].rearrange("p a s -> p (a s)"),
                                      start=(k == 0), stop=False)
                            ins = pe.matmul(out[:, 0:C_SLOTS], w[LO], xT[:, par, k, HI], start=False,
                                            stop=(k == KC - 1))
                    ins.then_inc(pe_f, 1)

            def down(e, par):
                wait(pe, dve_wd, e + 1)
                wait(pe, pool_w, e + 1)
                wait(pe, dve_h, e + 1)
                for h in range(2):
                    wait(pe, act_y, 2 * (e - 1) + h + 1)
                    for ic in range(IC):
                        at = ic * C_SLOTS + h * HALF
                        for a, b in PASSES:
                            ins = pe.matmul(p_y[0:HALF, h], hb[:, par, a, at:at + HALF], down_of(par, b)[:, ic],
                                            start=(ic == 0 and (a, b) == PASSES[0]),
                                            stop=(ic == IC - 1 and (a, b) == PASSES[-1]))
                    ins.then_inc(pe_y, 1)

            def body(e, par):
                if there(e + 2):
                    transposes(e + 2, par)
                if there(e + 1):
                    gate_up(e + 1, 1 - par)
                down(e, par)

            transposes(0, 0)
            gate_up(0, 0)
            transposes(1, 1)
            by_pairs(pe, body)


def last_norm(nc, acc, out):
    N, D = acc.shape
    HT = NB // P
    TT = 2 * HT
    TURNS = N // (2 * NB)
    with ExitStack() as ctx:
        def sb(name, shape, dt=F32):
            return ctx.enter_context(nc.sbuf_tensor(name, shape, dt))

        rows = sb("a_rows", [P, 2 * TURNS, HT, D])
        scale = sb("a_scale", [P, TURNS, TT])
        shift = sb("a_shift", [P, TURNS, TT])
        bn = sb("lbn", [P, TT, 6])
        mv = sb("lmv", [P, TT, 2])
        small = sb("lsmall", [P, 3, TT])
        spare = sb("lspare", [P, 1])
        loaded = [ctx.enter_context(nc.semaphore(f"l_in{h}")) for h in range(2)]
        stored = ctx.enter_context(nc.semaphore("l_out"))
        ln_c = ctx.enter_context(nc.semaphore("l_c"))
        dve_s = ctx.enter_context(nc.semaphore("l_s"))
        act_o = ctx.enter_context(nc.semaphore("l_o"))

        acc_v = acc.rearrange("(c j p) d -> p c j d", p=P, j=HT)
        out_v = out.rearrange("b s d -> (b s) d").rearrange("(c j p) d -> p c j d", p=P, j=HT)
        block = ctx.enter_context(nc.Block())

        def half(view, c, h):
            return view[:, bass.ds(2 * c + h, 1)].rearrange("p o j d -> p (o j) d")

        @block.sync
        def _(sp):
            def load(c, h):
                sp.dma_start(half(rows, c, h), half(acc_v, c, h)).then_inc(loaded[h], 16)

            load(0, 0)
            load(0, 1)
            with sp.Fori(1, TURNS) as c:
                for h in range(2):
                    wait(sp, loaded[h], 16 * c)
                    load(c, h)

        @block.vector
        def _(dve):
            link = Chain(dve, ln_c, 2 * TT + 3 + 3 * NEWTON)
            with dve.Fori(0, TURNS) as c:
                link.turn(c)
                for h in range(2):
                    wait(dve, loaded[h], 16 * (c + 1))
                    for j in range(HT):
                        link.then(dve.bn_stats(bn[:, h * HT + j], half(rows, c, h)[:, j]))
                link.settle_idle(spare[:])
                for j in range(TT):
                    link.then(dve.bn_aggr(mv[:, j], bn[:, j]))
                link.settle()
                ln_rsqrt(dve, link, 1e-5, mv[:, :, 1], small[:, 0], small[:, 1], small[:, 2])
                this = bass.ds(c, 1)
                dve.tensor_copy(scale[:, this].rearrange("p o j -> p (o j)"), small[:, 1])
                dve.scalar_tensor_tensor(out=shift[:, this].rearrange("p o j -> p (o j)"), in0=mv[:, :, 0],
                                         scalar=-1.0, in1=small[:, 1], op0=ALU.mult, op1=ALU.mult)\
                    .then_inc(dve_s, 1)
                link.close()

        @block.scalar
        def _(act):
            with act.Fori(0, TURNS) as c:
                wait(act, dve_s, c + 1)
                this = bass.ds(c, 1)
                for h in range(2):
                    for j in range(HT):
                        row = half(rows, c, h)[:, j]
                        act.activation(row, row, ACT.Identity, bias=shift[:, this, h * HT + j],
                                       scale=scale[:, this, h * HT + j]).then_inc(act_o, 1)
                    wait(act, act_o, TT * c + HT * (h + 1))
                    act.dma_start(half(out_v, c, h), half(rows, c, h)).then_inc(stored, 16)
            act.wait_ge(stored, 16 * 2 * TURNS)


N_EXPERTS_FACTOR = (5, 4)


def build(nc, x, xT, w_qkv, w_o, router_wT, e_bias, w_gate, w_up, w_down, gate_T, up_T, down_T, out):
    B, S, D = x.shape
    N, E = B * S, w_gate.shape[0]
    a, b = N_EXPERTS_FACTOR
    c_slots = -(-a * N // (b * E))

    def scratch(name, shape):
        return nc.dram_tensor(name, shape, F32, kind="Internal").ap()

    y, x2, acc = (scratch(n, (N, D)) for n in ("y_rows", "x2_rows", "acc_rows"))
    table = scratch("slot_table", (E * c_slots, 2))
    weights = (w_gate, w_up, w_down)
    with ExitStack() as ctx:
        norm1 = Norm1(nc, ctx, x.shape[2])
        attention(nc, norm1, x, xT, w_qkv, w_o, y)
        ready = Handover(nc, ctx, E, x.shape[2], w_gate.shape[2], c_slots)
        route_and_share(nc, norm1, ready, y, router_wT, e_bias, gate_T, up_T, down_T, weights, x2, acc, table, c_slots)
        experts(nc, ready, weights, x2, acc, c_slots)
    last_norm(nc, acc, out)


def kernel(**inputs):
    import numpy as _np
    import concourse.bacc as _bacc
    from concourse import mybir as _mybir
    from concourse.bass_utils import run_bass_kernel_spmd as _run

    nc = _bacc.Bacc("TRN2", target_bir_lowering=False, num_devices=1)
    given = {k: _np.asarray(v) for k, v in inputs.items()}
    x = given["L0_attn_x"]
    laid_out = {
        "x": x,
        "xT": x.reshape(-1, x.shape[-1]).T,
        "w_qkv": given["L0_attn_w_qkv"],
        "w_o": given["L0_attn_w_o"],
        "router_wT": given["L0_ffn_router_w"].T,
        "e_bias": given["L0_ffn_e_bias"],
        "w_gate": given["L0_ffn_W_gate"],
        "w_up": given["L0_ffn_W_up"],
        "w_down": given["L0_ffn_W_down"],
        "gate_T": given["L0_ffn_shared_gate"].T,
        "up_T": given["L0_ffn_shared_up"].T,
        "down_T": given["L0_ffn_shared_down"].T,
    }
    arrays, args = {}, []
    for name, a in laid_out.items():
        a = _np.ascontiguousarray(a)
        arrays[f"in_{name}"] = a
        args.append(nc.dram_tensor(f"in_{name}", a.shape, _mybir.dt.from_np(a.dtype), kind="ExternalInput").ap())
    args.append(nc.dram_tensor("out_rows", x.shape, F32, kind="ExternalOutput").ap())
    build(nc, *args)
    r = _run(nc, [arrays], core_ids=[0])
    return r.results[0]["out_rows"]
```
